# Optimizing a Trainium2 kernel written in Bass

```python
import numpy as np
import jax
import jax.numpy as jnp

def _softmax(x, axis=-1):
    return jax.nn.softmax(x, axis=axis)
def _gelu(x):
    return jax.nn.gelu(x, approximate=True)
def _silu(x):
    return jax.nn.silu(x)
def _sigmoid(x):
    return jax.nn.sigmoid(x)
def _layernorm(x, axis=-1, eps=1e-5):
    m = jnp.mean(x, axis=axis, keepdims=True)
    v = jnp.var(x, axis=axis, keepdims=True)
    return (x - m) / jnp.sqrt(v + eps)
def _scatter_add(tgt, idx, src, axis=0):
    return tgt.at[idx].add(src)
def _segment_sum(src, seg, n):
    return jax.ops.segment_sum(src, seg, n)

kernel_name = 'mk_conv_preact_d2_conv_nchw256_0a9304'

def setup_inputs(seed: int = 0):
    np.random.seed(seed)
    _w = jnp.asarray
    def _rec_inputs():
        import jax
        import jax.numpy as jnp
        _gk = jax.random.key(seed)
        x = -0.0003957 + 1 * jax.random.normal(jax.random.fold_in(_gk, 1), (16, 256, 56, 56), jnp.float32)
        return x
    x = _rec_inputs()
    def _L0_conv_setup():
        import jax, jax.numpy as jnp
        import numpy as np
        GROUPS = 16
        GROUP_SIZE = 16
        K = 3
        KK = K * K
        BN_EPS = 1e-05
        key = jax.random.key(seed)
        ks = jax.random.split(key, 6)
        B, C, H, W = (16, 256, 56, 56)
        mid = C // 4
        x = jax.random.normal(ks[0], (B, C, H, W), dtype=jnp.float32)
        w1 = jax.random.normal(ks[1], (mid, C), dtype=jnp.float32) * (1.0 / np.sqrt(C))
        bn_gamma = jnp.ones((mid,), dtype=jnp.float32)
        bn_beta = jnp.zeros((mid,), dtype=jnp.float32)
        bn_mean = jax.random.normal(ks[2], (mid,), dtype=jnp.float32) * 0.1
        bn_var = jax.random.uniform(ks[3], (mid,), dtype=jnp.float32, minval=0.5, maxval=1.5)
        w2 = jax.random.normal(ks[4], (KK * GROUPS, mid), dtype=jnp.float32) * (1.0 / np.sqrt(mid))
        b2 = jax.random.normal(ks[5], (KK * GROUPS,), dtype=jnp.float32) * 0.01
        return {'x': x, 'w1': w1, 'bn_gamma': bn_gamma, 'bn_beta': bn_beta, 'bn_mean': bn_mean, 'bn_var': bn_var, 'w2': w2, 'b2': b2}
    _L0_conv_all = _L0_conv_setup()
    _L0_conv_in = {k: v for k, v in _L0_conv_all.items() if k in ('w1', 'bn_gamma', 'bn_beta', 'bn_mean', 'bn_var', 'w2', 'b2', )}
    del _L0_conv_all

    def _L1_conv_setup():
        import jax, jax.numpy as jnp
        import numpy as np
        C_OUT, C_IN, K = (256, 256, 3)
        STRIDE, PAD = (1, 1)

        def _binary_conv(x, weights):
            real_w = weights.reshape(C_OUT, C_IN, K, K)
            scale = jax.lax.stop_gradient(jnp.mean(jnp.abs(real_w), axis=(1, 2, 3), keepdims=True))
            bin_no_grad = scale * jnp.sign(real_w)
            clipped = jnp.clip(real_w, -1.0, 1.0)
            bin_w = jax.lax.stop_gradient(bin_no_grad - clipped) + clipped
            return jax.lax.conv_general_dilated(x, bin_w, window_strides=(STRIDE, STRIDE), padding=[(PAD, PAD), (PAD, PAD)], dimension_numbers=('NCHW', 'OIHW', 'NCHW'))
        key = jax.random.key(seed)
        kx, kw = jax.random.split(key)
        x = jax.random.normal(kx, (32, C_IN, 56, 56), dtype=jnp.float32)
        weights = jax.random.uniform(kw, (C_OUT * C_IN * K * K, 1), dtype=jnp.float32) * 0.001
        return {'x': x, 'weights': weights}
    _L1_conv_all = _L1_conv_setup()
    _L1_conv_in = {k: v for k, v in _L1_conv_all.items() if k in ('weights', )}
    del _L1_conv_all

    return {
        "x": x,
        "L0_conv_w1": _L0_conv_in["w1"],
        "L0_conv_bn_gamma": _L0_conv_in["bn_gamma"],
        "L0_conv_bn_beta": _L0_conv_in["bn_beta"],
        "L0_conv_bn_mean": _L0_conv_in["bn_mean"],
        "L0_conv_bn_var": _L0_conv_in["bn_var"],
        "L0_conv_w2": _L0_conv_in["w2"],
        "L0_conv_b2": _L0_conv_in["b2"],
        "L1_conv_weights": _L1_conv_in["weights"],
    }

def reference(x, L0_conv_w1, L0_conv_bn_gamma, L0_conv_bn_beta, L0_conv_bn_mean, L0_conv_bn_var, L0_conv_w2, L0_conv_b2, L1_conv_weights):
    import jax
    import jax.numpy as jnp
    def _L0_conv_ref(x, w1, bn_gamma, bn_beta, bn_mean, bn_var, w2, b2):
        import jax, jax.numpy as jnp
        import numpy as np
        GROUPS = 16
        GROUP_SIZE = 16
        K = 3
        KK = K * K
        BN_EPS = 1e-05
        B, C, H, W = x.shape
        t = jnp.einsum('bchw,oc->bohw', x, w1)
        scale = bn_gamma / jnp.sqrt(bn_var + BN_EPS)
        t = t * scale[None, :, None, None] + (bn_beta - bn_mean * scale)[None, :, None, None]
        t = jax.nn.relu(t)
        weight = jnp.einsum('bchw,oc->bohw', t, w2) + b2[None, :, None, None]
        weight = weight.reshape(B, GROUPS, 1, KK, H, W)
        xp = jnp.pad(x, ((0, 0), (0, 0), (1, 1), (1, 1)))
        patches = jnp.stack([xp[:, :, i:i + H, j:j + W] for i in range(K) for j in range(K)], axis=2)
        patches = patches.reshape(B, GROUPS, GROUP_SIZE, KK, H, W)
        out = (weight * patches).sum(axis=3).reshape(B, C, H, W)
        return out

    def _L1_conv_ref(x, weights):
        import jax, jax.numpy as jnp
        import numpy as np
        C_OUT, C_IN, K = (256, 256, 3)
        STRIDE, PAD = (1, 1)

        def _binary_conv(x, weights):
            real_w = weights.reshape(C_OUT, C_IN, K, K)
            scale = jax.lax.stop_gradient(jnp.mean(jnp.abs(real_w), axis=(1, 2, 3), keepdims=True))
            bin_no_grad = scale * jnp.sign(real_w)
            clipped = jnp.clip(real_w, -1.0, 1.0)
            bin_w = jax.lax.stop_gradient(bin_no_grad - clipped) + clipped
            return jax.lax.conv_general_dilated(x, bin_w, window_strides=(STRIDE, STRIDE), padding=[(PAD, PAD), (PAD, PAD)], dimension_numbers=('NCHW', 'OIHW', 'NCHW'))
        return _binary_conv(x, weights)

    def _gn(v, G=32, eps=1e-5):
        B_, C_, H_, W_ = v.shape
        g = v.reshape(B_, G, C_ // G, H_, W_)
        m = jnp.mean(g, axis=(2, 3, 4), keepdims=True)
        s = jnp.var(g, axis=(2, 3, 4), keepdims=True)
        return ((g - m) / jnp.sqrt(s + eps)).reshape(v.shape)

    def _ln_c(v, eps=1e-6):
        m = jnp.mean(v, axis=1, keepdims=True)
        s = jnp.var(v, axis=1, keepdims=True)
        return (v - m) / jnp.sqrt(s + eps)

    def _ln_t(v, eps=1e-5):
        m = jnp.mean(v, axis=-1, keepdims=True)
        s = jnp.var(v, axis=-1, keepdims=True)
        return (v - m) / jnp.sqrt(s + eps)

    def _to_tokens(v):
        B_, C_, H_, W_ = v.shape
        return v.reshape(B_, C_, H_ * W_).transpose(0, 2, 1)
    def _from_tokens(t, like):
        B_, C_, H_, W_ = like.shape
        return t.transpose(0, 2, 1).reshape(B_, C_, H_, W_)

    x = x + _L0_conv_ref(_gn(x), L0_conv_w1, L0_conv_bn_gamma, L0_conv_bn_beta, L0_conv_bn_mean, L0_conv_bn_var, L0_conv_w2, L0_conv_b2)
    x = x + _L1_conv_ref(_gn(x), L1_conv_weights)
    return x


_drawn_inputs = setup_inputs


def setup_inputs(seed=0):
    import zlib

    import numpy as np

    out = dict(_drawn_inputs(seed))
    spreads = {'L0_conv_bn_gamma': (1.0, 0.2), 'L0_conv_bn_beta': (0.0, 0.1)}
    factors = {'L0_conv_b2': 4.909, 'L1_conv_weights': 8.0}
    for name, (base, spread) in spreads.items():
        noise = np.random.default_rng([zlib.crc32(name.encode()), seed]).standard_normal(out[name].shape)
        drawn = base * np.exp(spread * noise) if base else spread * noise
        out[name] = jnp.asarray(drawn.astype(out[name].dtype))
    for name, factor in factors.items():
        out[name] = (out[name] * factor).astype(out[name].dtype)
    return out
```

```python
from contextlib import ExitStack

import concourse.bass as bass
from concourse import mybir

F32 = mybir.dt.float32
F16 = mybir.dt.float16
ALU = mybir.AluOpType
ACT = mybir.ActivationFunctionType

P = 128
KT = 2
H = W = 56
ROWS = 8
BLK = ROWS * W
NB = H // ROWS
PIX = H * W
HP = H + 2
TAPS = 9
MID = 64
GROUPS = 16
WROWS = 2 * GROUPS
TPT = 3
WT = TAPS // TPT
GN_EPS = 1e-5
BN_EPS = 1e-5
LOSCALE = 2048.0
RING = 3
CONV_LAG = 2
STEPS = 15


def later(value):
    return not isinstance(value, int) or value > 0


class Image:

    def __init__(self, n, parity, here=True, after=True, before=True, before2=True):
        self.n, self.parity = n, parity
        self.here, self.after, self.before, self.before2 = here, after, before, before2


def program(nc, x, w1t, bn, w2t, conv_w, conv_sel, group_avg, row_scales, out):
    B = x.shape[0]
    pairs = (B - 4) // 2
    assert B % 2 == 0 and B >= 4

    def iterations(eng, step):
        def fixed(n):
            step(Image(n, n % 2, n < B, n + 1 < B, 1 <= n <= B, 2 <= n))
        fixed(0)
        fixed(1)
        if pairs > 0:
            with eng.Fori(0, pairs) as i:
                step(Image(i * 2 + 2, 0))
                step(Image(i * 2 + 3, 1))
        for n in range(2 + 2 * max(pairs, 0), B + 2):
            fixed(n)

    x_dram = x.rearrange("b (t p) s -> b p t s", p=P)
    out_dram = out.rearrange("b (t p) s -> b p t s", p=P)

    with ExitStack() as ctx:
        def sb(name, shape, dt=F32):
            return ctx.enter_context(nc.sbuf_tensor(name, shape, dt))

        def sem(name):
            return ctx.enter_context(nc.semaphore(name))

        X = sb("X", [P, 2, KT, PIX])
        X1 = sb("X1", [P, 2, KT, PIX])
        XN = sb("XN", [P, KT, HP, HP])
        HL = sb("HL", [P, 2, HP, KT, HP], F16)
        PROD = sb("PROD", [P, RING, KT, BLK])
        TS = sb("TS", [P, 2, ROWS, KT, W])
        T = sb("T", [MID + 1, 2, BLK])
        WH = sb("WH", [TPT * WROWS, 2, BLK], F16)
        WZ = sb("WZ", [TPT * WROWS, 2, WT, BLK], F16)
        CW = sb("CW", [P, 2, KT, TAPS, KT * P], F16)
        W1 = sb("W1", [P, KT, MID])
        W2 = sb("W2", [MID + 1, TAPS, WROWS])
        SEL = sb("SEL", [TPT * WROWS, KT, P], F16)
        GAVG = sb("GAVG", [P, P])
        RSC = sb("RSC", [TPT * WROWS, 2])
        BN = sb("BN", [MID, 4])
        BNF = sb("BNF", [MID, 6])
        ONES = sb("ONES", [P, 1])
        CSC = sb("CSC", [P, KT])
        RAW = sb("RAW", [P, 2, KT, NB, 6])
        AGG = sb("AGG", [P, 2, KT, 2])
        MSQ = sb("MSQ", [P, 2, KT])
        GRP = sb("GRP", [P, 2, KT, 2])
        VAR = sb("VAR", [P, 2, KT])
        SD = sb("SD", [P, 2, KT])
        RS0 = sb("RS0", [P, 2, KT])
        TMP = sb("TMP", [P, 2, KT])
        NORM = sb("NORM", [P, 2, 2, 2, KT])
        NORM_LO = sb("NORM_LO", [P, 2, 2, KT])
        PS = ctx.enter_context(nc.psum_tensor("PS", [P, 8, 512], F32))
        HID, WTILE, BCAST, CONV = 0, 1, 2, 6
        STAT = slice(BLK, BLK + 2 * KT)

        x_loaded = [sem(f"x_loaded{t}") for t in range(KT)]
        consts_loaded = sem("consts_loaded")
        convw_loaded = sem("convw_loaded")
        border_ready = sem("border_ready")
        consts_ready = sem("consts_ready")
        bn_sqrt = sem("bn_sqrt")
        signs_ready = sem("signs_ready")
        abs_ready = sem("abs_ready")
        abs_summed = sem("abs_summed")
        chain = [sem("x_chain"), sem("x1_chain")]
        var_step = [sem("x_var_step"), sem("x1_var_step")]
        bias_step = sem("bias_step")
        group_sum = [sem("x_group_sum"), sem("x1_group_sum")]
        sd_ready = [sem("x_sd_ready"), sem("x1_sd_ready")]
        xn_ready = sem("xn_ready")
        hidden_done = sem("hidden_done")
        t_ready = sem("t_ready")
        tile_done = sem("tile_done")
        high_ready = sem("high_ready")
        z_ready = sem("z_ready")
        bcast_done = sem("bcast_done")
        prod_done = sem("prod_done")
        added = sem("added")
        split_ready = sem("split_ready")
        low_ready = sem("low_ready")
        conv_done = sem("conv_done")
        final_done = sem("final_done")
        stored = [sem(f"stored{j}") for j in range(NB)]

        CONSTS = 6

        def rows_of(j):
            return slice(1 + ROWS * j, 1 + ROWS * (j + 1))

        def cols_of(j):
            return slice(BLK * j, BLK * (j + 1))

        def grid(ap):
            return ap.rearrange("p (r c) -> p r c", c=W)

        def conv_block(im, j):
            if j >= CONV_LAG:
                return (im.n - 1, 1 - im.parity, j - CONV_LAG) if im.before else None
            return (im.n - 2, im.parity, j + NB - CONV_LAG) if im.before2 else None

        def last_conv_block(im, j):
            if j >= 1:
                return conv_block(im, j - 1)
            return (im.n - 2, im.parity, NB - 1 - CONV_LAG) if im.before2 else None

        def next_block(im, j):
            if j + 1 < NB:
                return (im.n, im.parity, j + 1) if im.here else None
            return (im.n + 1, 1 - im.parity, 0) if im.after else None

        def norm_block(im, j):
            if j < NB - 2:
                return (im.n, im.parity, j + 2) if im.here else None
            return (im.n + 1, 1 - im.parity, j - (NB - 2)) if im.after else None

        block = ctx.enter_context(nc.Block())

        @block.sync
        def _(sp):
            def load_image(n, parity):
                for t in range(KT):
                    src = x_dram[n] if isinstance(n, int) else x_dram[bass.ds(n, 1)].rearrange("a p t s -> (a p) t s")
                    sp.dma_start(X[:, parity, t, :], src[:, t, :]).then_inc(x_loaded[t], 16)

            load_image(0, 0)
            sp.dma_start(GAVG[:, :], group_avg).then_inc(consts_loaded, 16)
            sp.dma_start(W1[:, :, :], w1t).then_inc(consts_loaded, 16)
            sp.dma_start(BN[:, :], bn).then_inc(consts_loaded, 16)
            sp.dma_start(W2[:, :, :], w2t).then_inc(consts_loaded, 16)
            sp.dma_start(SEL[:, :, :], conv_sel).then_inc(consts_loaded, 16)
            sp.dma_start(RSC[:, :], row_scales).then_inc(consts_loaded, 16)
            sp.dma_start(X1[:, 1, :, :].rearrange("p t s -> p (t s)")[:, 0:KT * TAPS * KT * P], conv_w
                         ).then_inc(convw_loaded, 16)

            def step(im):
                for j in range(NB):
                    c = last_conv_block(im, j)
                    if c:
                        n, parity, b = c
                        if later(n):
                            sp.wait_ge(stored[b], n * 16)
                        sp.wait_ge(final_done, (n * NB + b + 1) * KT)
                        dst = out_dram[n] if isinstance(n, int) else out_dram[bass.ds(n, 1)].rearrange("a p t s -> (a p) t s")
                        sp.dma_start(dst[:, :, cols_of(b)], X1[:, parity, :, cols_of(b)]).then_inc(stored[b], 16)
                    if j == 0 and im.after:
                        if later(im.n):
                            sp.wait_ge(added, im.n * (NB * TAPS))
                        sp.wait_ge(chain[0], im.n * STEPS + 2)
                        load_image(im.n + 1, 1 - im.parity)

            iterations(sp, step)
            for b in range(NB):
                sp.wait_ge(stored[b], 16 * B)

        @block.gpsimd
        def _(pool):
            pool.memset(HL[:, :, :, :, :].rearrange("p h r t c -> p (h r t c)").bitcast(F32), 0.0).then_inc(border_ready, 1)

            def step(im):
                if not im.here:
                    return
                n, parity = im.n, im.parity
                for j in range(NB):
                    for k in range(TAPS):
                        done = (n * NB + j) * TAPS + k
                        if k == 0:
                            if later(n - 1):
                                pool.wait_ge(stored[j], (n - 1) * 16)
                            if isinstance(n, int) and n == 1 and j == 0:
                                pool.wait_ge(abs_summed, 2)
                        if later(done):
                            pool.wait_ge(added, done)
                        pool.wait_ge(prod_done, done + 1)
                        acc = X1[:, parity, :, cols_of(j)]
                        before = X[:, parity, :, cols_of(j)] if k == 0 else acc
                        pool.tensor_tensor(acc, before, PROD[:, k % RING, :, :], ALU.add).then_inc(added, 1)

            iterations(pool, step)

        @block.scalar
        def _(act):
            def normalise(n, parity, b):
                if b == 0 or (b == 1 and isinstance(n, int) and n == 0):
                    act.wait_ge(chain[0], (n + 1) * STEPS)
                last_reader = (n - 1) * NB + min(b + 1, NB - 1) + 1
                if later(last_reader):
                    act.wait_ge(prod_done, last_reader * TAPS)
                for t in range(KT):
                    ins = act.activation(XN[:, t, rows_of(b), 1:1 + W], grid(X[:, parity, t, cols_of(b)]), ACT.Identity,
                                         bias=NORM[:, 0, parity, 1, t:t + 1], scale=NORM[:, 0, parity, 0, t:t + 1])
                ins.then_inc(xn_ready, 1)

            def hidden(g, buf):
                act.wait_ge(hidden_done, g + 1)
                if later(g - 1):
                    act.wait_ge(tile_done, (g - 1) * WT)
                act.activation(T[0:MID, buf, :], PS[0:MID, HID, 0:BLK], ACT.Relu, bias=BNF[:, 5:6],
                               scale=BNF[:, 3:4]).then_inc(t_ready, 1)

            def high(g, i, buf):
                act.wait_ge(tile_done, g * WT + i + 1)
                if later(g * WT + i - 1):
                    act.wait_ge(z_ready, g * WT + i - 1)
                act.activation(WH[:, buf, :], PS[0:TPT * WROWS, WTILE, 0:BLK], ACT.Identity,
                               bias=0.0, scale=RSC[:, 0:1]).then_inc(high_ready, 1)

            def split(n, parity, b):
                if b == 0:
                    act.wait_ge(chain[1], (n + 1) * STEPS)
                g = n * NB + b
                if later(g - 1):
                    act.wait_ge(low_ready, g - 1)
                last_reader = (n - 1) * NB + min(b + 1, NB - 1) + 1
                if later(last_reader):
                    act.wait_ge(conv_done, last_reader * KT)
                buf = (parity + b) % 2
                for t in range(KT):
                    src = grid(X1[:, parity, t, cols_of(b)])
                    act.activation(TS[:, buf, :, t, :], src, ACT.Identity, bias=NORM_LO[:, parity, 1, t:t + 1],
                                   scale=NORM_LO[:, parity, 0, t:t + 1])
                    ins = act.activation(HL[:, 0, rows_of(b), t, 1:1 + W], src, ACT.Identity,
                                         bias=NORM[:, 1, parity, 1, t:t + 1], scale=NORM[:, 1, parity, 0, t:t + 1])
                ins.then_inc(split_ready, 1)

            def root(kind, n, step_of_var):
                act.wait_ge(chain[kind], n * STEPS + step_of_var)
                act.activation(SD[:, kind, :], VAR[:, kind, :], ACT.Sqrt).then_inc(sd_ready[kind], 1)

            act.wait_ge(consts_ready, 1)
            act.activation(BNF[:, 1:2], BNF[:, 0:1], ACT.Sqrt).then_inc(bn_sqrt, 1)
            root(0, 0, 9)
            act.wait_ge(border_ready, 3)
            normalise(0, 0, 0)
            normalise(0, 0, 1)
            act.wait_ge(consts_ready, 6)
            hidden(0, 0)
            for i in range(WT):
                high(0, i, i % 2)

            def step(im):
                for j in range(NB):
                    nxt = next_block(im, j)
                    if nxt:
                        n, parity, b = nxt
                        g, buf = n * NB + b, (parity + b) % 2
                        hidden(g, buf)
                    if norm_block(im, j):
                        normalise(*norm_block(im, j))
                    if nxt:
                        high(g, 0, buf)
                    if im.before and j >= 1:
                        split(im.n - 1, 1 - im.parity, 0 if j == 1 else j)
                    if nxt:
                        high(g, 1, (buf + 1) % 2)
                    if im.before and j == 1:
                        split(im.n - 1, 1 - im.parity, 1)
                    if j == 4 and im.after:
                        root(0, im.n + 1, 9)
                    if nxt:
                        high(g, 2, buf)
                    if j == 0 and im.before:
                        root(1, im.n - 1, 9)
                    if j == 3 and isinstance(im.n, int) and im.n == 0:
                        act.wait_ge(signs_ready, 2)
                        wraw = X1[:, 1, :, :].rearrange("p t s -> p (t s)")[:, 0:KT * TAPS * KT * P]
                        act.activation(wraw, wraw, ACT.Abs).then_inc(abs_ready, 1)

            iterations(act, step)

        @block.vector
        def _(dve):
            def link(ins, kind, value):
                ins.then_inc(chain[kind], 1)
                dve.wait_ge(chain[kind], value)

            def partial_stats(kind, src, t, b):
                dve.bn_stats(RAW[:, kind, t, b, :], src[:, cols_of(b)])

            def channel_stats(kind, n):
                s = n * STEPS
                for t in range(KT):
                    dve.bn_aggr(AGG[:, kind, t, :], RAW[:, kind, t, :, :].rearrange("p b s -> p (b s)")
                                ).then_inc(chain[kind], 1)
                dve.wait_ge(chain[kind], s + 4)
                link(dve.tensor_tensor(MSQ[:, kind, :], AGG[:, kind, :, 0], AGG[:, kind, :, 0], ALU.mult), kind, s + 5)
                dve.tensor_tensor(AGG[:, kind, :, 1], AGG[:, kind, :, 1], MSQ[:, kind, :], ALU.add).then_inc(chain[kind], 1)

            def group_variance(kind, n):
                s = n * STEPS
                dve.wait_ge(group_sum[kind], n + 1)
                link(dve.tensor_copy(GRP[:, kind, :, :].rearrange("p t s -> p (t s)"), PS[:, HID, STAT]), kind, s + 7)
                link(dve.tensor_tensor(MSQ[:, kind, :], GRP[:, kind, :, 0], GRP[:, kind, :, 0], ALU.mult), kind, s + 8)
                dve.tensor_tensor(TMP[:, kind, :], GRP[:, kind, :, 1], MSQ[:, kind, :], ALU.subtract).then_inc(var_step[kind], 1)
                dve.wait_ge(var_step[kind], n + 1)
                dve.tensor_scalar(VAR[:, kind, :], TMP[:, kind, :], 0.0, GN_EPS, ALU.max, ALU.add).then_inc(chain[kind], 1)

            def scale_and_bias(kind, n, parity):
                s = n * STEPS
                scale, bias = NORM[:, kind, parity, 0, :], NORM[:, kind, parity, 1, :]
                dve.wait_ge(sd_ready[kind], n + 1)
                link(dve.reciprocal(RS0[:, kind, :], SD[:, kind, :]), kind, s + 10)
                link(dve.tensor_tensor(TMP[:, kind, :], RS0[:, kind, :], RS0[:, kind, :], ALU.mult), kind, s + 11)
                link(dve.tensor_tensor(TMP[:, kind, :], TMP[:, kind, :], VAR[:, kind, :], ALU.mult), kind, s + 12)
                link(dve.tensor_scalar(TMP[:, kind, :], TMP[:, kind, :], -0.5, 1.5, ALU.mult, ALU.add), kind, s + 13)
                link(dve.tensor_tensor(scale, RS0[:, kind, :], TMP[:, kind, :], ALU.mult), kind, s + 14)
                bias_ins = dve.scalar_tensor_tensor(out=bias, in0=GRP[:, kind, :, 0], scalar=-1.0, in1=scale,
                                                    op0=ALU.mult, op1=ALU.mult)
                if kind == 0:
                    bias_ins.then_inc(chain[0], 1)
                else:
                    bias_ins.then_inc(bias_step, 1)
                    dve.wait_ge(bias_step, n + 1)
                    dve.tensor_scalar(NORM_LO[:, parity, :, :], NORM[:, 1, parity, :, :], LOSCALE, None,
                                      ALU.mult).then_inc(chain[1], 1)

            def product(g, parity, j, k):
                n_done = g * TAPS + k
                dve.wait_ge(bcast_done, n_done + 1)
                if later(n_done + 1 - RING):
                    dve.wait_ge(added, n_done + 1 - RING)
                bank = BCAST + 2 * ((parity + j + k) % 2)
                di, dj = divmod(k, 3)
                shifted = XN[:, :, ROWS * j + di:ROWS * j + di + ROWS, dj:dj + W]
                dve.tensor_tensor(PROD[:, k % RING, :, :].rearrange("p t (r c) -> p t r c", c=W),
                                  PS[:, bank:bank + 2, 0:BLK].rearrange("p t (r c) -> p t r c", c=W),
                                  shifted, ALU.mult).then_inc(prod_done, 1)

            def low_rows(g, i, buf):
                dve.wait_ge(high_ready, g * WT + i + 1)
                dve.scalar_tensor_tensor(out=WZ[:, buf, i, :], in0=WH[:, (buf + i) % 2, :], scalar=RSC[:, 1:2],
                                         in1=PS[0:TPT * WROWS, WTILE, 0:BLK], op0=ALU.mult,
                                         op1=ALU.add).then_inc(z_ready, 1)

            def low_half(n, parity, b):
                dve.wait_ge(split_ready, n * NB + b + 1)
                high_half = HL[:, 0, rows_of(b), :, 1:1 + W].rearrange("p r t c -> p (r t) c")
                dve.scalar_tensor_tensor(out=HL[:, 1, rows_of(b), :, 1:1 + W].rearrange("p r t c -> p (r t) c"),
                                         in0=high_half, scalar=-LOSCALE,
                                         in1=TS[:, (parity + b) % 2, :, :, :].rearrange("p r t c -> p (r t) c"),
                                         op0=ALU.mult, op1=ALU.add).then_inc(low_ready, 1)

            def residual(n, parity, b, t):
                dve.wait_ge(conv_done, (n * NB + b) * KT + t + 1)
                o = X1[:, parity, t, cols_of(b)]
                dve.scalar_tensor_tensor(out=o, in0=PS[:, CONV + t, 0:BLK], scalar=CSC[:, t:t + 1], in1=o,
                                         op0=ALU.mult, op1=ALU.add).then_inc(final_done, 1)

            dve.memset(XN[:, :, :, :], 0.0).then_inc(border_ready, 1)
            dve.memset(T[MID:MID + 1, :, :], 1.0)
            dve.memset(ONES[:, :], 1.0).then_inc(border_ready, 1)
            for t in range(KT):
                dve.wait_ge(x_loaded[t], 16)
                for b in range(NB):
                    ins = dve.bn_stats(RAW[:, 0, t, b, :], X[:, 0, t, cols_of(b)])
                ins.then_inc(chain[0], 1)
            dve.wait_ge(chain[0], 2)
            channel_stats(0, 0)
            dve.wait_ge(consts_loaded, 16 * CONSTS)
            dve.tensor_scalar(BNF[:, 0:1], BN[:, 3:4], BN_EPS, None, ALU.add).then_inc(consts_ready, 1)
            dve.wait_ge(bn_sqrt, 1)
            dve.reciprocal(BNF[:, 2:3], BNF[:, 1:2]).then_inc(consts_ready, 1)
            dve.wait_ge(consts_ready, 2)
            dve.tensor_tensor(BNF[:, 3:4], BN[:, 0:1], BNF[:, 2:3], ALU.mult).then_inc(consts_ready, 1)
            dve.wait_ge(consts_ready, 3)
            dve.tensor_tensor(BNF[:, 4:5], BN[:, 2:3], BNF[:, 3:4], ALU.mult).then_inc(consts_ready, 1)
            dve.wait_ge(consts_ready, 4)
            dve.tensor_tensor(BNF[:, 5:6], BN[:, 1:2], BNF[:, 4:5], ALU.subtract).then_inc(consts_ready, 1)
            dve.tensor_scalar(W2[:, :, GROUPS:WROWS], W2[:, :, GROUPS:WROWS], LOSCALE, None, ALU.mult).then_inc(consts_ready, 1)
            group_variance(0, 0)
            scale_and_bias(0, 0, 0)
            for i in range(WT):
                low_rows(0, i, 0)

            def take_signs():
                dve.wait_ge(convw_loaded, 16)
                wraw = X1[:, 1, :, :].rearrange("p t s -> p (t s)")[:, 0:KT * TAPS * KT * P]
                hi = CW[:, 0, :, :, :].rearrange("p t k o -> p (t k o)")
                lo = CW[:, 1, :, :, :].rearrange("p t k o -> p (t k o)")
                dve.tensor_scalar(hi, wraw, 0.0, None, ALU.is_lt).then_inc(signs_ready, 1)
                dve.wait_ge(signs_ready, 1)
                dve.scalar_tensor_tensor(out=hi, in0=wraw, scalar=0.0, in1=hi, op0=ALU.is_gt,
                                         op1=ALU.subtract).then_inc(signs_ready, 1)
                dve.wait_ge(signs_ready, 2)
                dve.tensor_scalar(lo, hi, 1.0 / LOSCALE, None, ALU.mult).then_inc(signs_ready, 1)

            def channel_scales():
                dve.wait_ge(abs_summed, 2)
                for t in range(KT):
                    ins = dve.tensor_scalar(CSC[:, t:t + 1], PS[:, CONV + t, 0:1], 1.0 / (KT * P * TAPS), None, ALU.mult)
                ins.then_inc(signs_ready, 1)
                dve.wait_ge(signs_ready, 4)

            def step(im):
                n, parity = im.n, im.parity
                todo = [(t, b) for t in range(KT) for b in range(NB)]
                for j in range(NB):
                    nxt = next_block(im, j)
                    for k in range(TAPS):
                        if im.here:
                            g = n * NB + j
                            if k == 0:
                                dve.wait_ge(xn_ready, n * NB + min(j + 1, NB - 1) + 1)
                        if k == 2 and j == 4 and im.after:
                            dve.wait_ge(chain[0], (n + 1) * STEPS + 2)
                        if k == 7 and j == 0 and im.before:
                            dve.wait_ge(chain[1], (n - 1) * STEPS + 2)
                        if im.here:
                            product(g, parity, j, k)
                        if k == 2 and j == 4 and im.after:
                            channel_stats(0, n + 1)
                        if k == 7 and j == 0 and im.before:
                            channel_stats(1, n - 1)
                        if k == 0 and j == 1 and im.before:
                            scale_and_bias(1, n - 1, 1 - parity)
                        if k == 0 and last_conv_block(im, j):
                            residual(*last_conv_block(im, j), 1)
                        if k in (1, 8) and 1 <= j <= 4 and im.after and todo:
                            for t, b in todo[:2]:
                                if b == 0:
                                    dve.wait_ge(x_loaded[t], (n + 2) * 16)
                                ins = dve.bn_stats(RAW[:, 0, t, b, :], X[:, 1 - parity, t, cols_of(b)])
                                if b == NB - 1:
                                    ins.then_inc(chain[0], 1)
                            todo = todo[2:]
                        if k == 3 and nxt:
                            low_rows(nxt[0] * NB + nxt[2], 0, (nxt[1] + nxt[2]) % 2)
                        if k == 4 and j >= 1 and im.before:
                            low_half(n - 1, 1 - parity, 0 if j == 1 else j)
                        if k == 5 and nxt:
                            low_rows(nxt[0] * NB + nxt[2], 1, (nxt[1] + nxt[2]) % 2)
                        if k == 5 and j == 4 and im.after:
                            group_variance(0, n + 1)
                        if k == 5 and conv_block(im, j):
                            residual(*conv_block(im, j), 0)
                        if k == 6:
                            c = (n, parity, j - 1) if j >= 1 and im.here else (n - 1, 1 - parity, NB - 1) if j == 0 and im.before else None
                            if c:
                                dve.wait_ge(added, (c[0] * NB + c[2] + 1) * TAPS)
                                for t in range(KT):
                                    ins = dve.bn_stats(RAW[:, 1, t, c[2], :], X1[:, c[1], t, cols_of(c[2])])
                                    if c[2] == NB - 1:
                                        ins.then_inc(chain[1], 1)
                        if k == 7 and nxt:
                            low_rows(nxt[0] * NB + nxt[2], 2, (nxt[1] + nxt[2]) % 2)
                        if k == 7 and j == 1 and im.before:
                            low_half(n - 1, 1 - parity, 1)
                        if k == 7 and j == 4 and im.after:
                            scale_and_bias(0, n + 1, 1 - parity)
                    if j == 0 and im.before:
                        group_variance(1, n - 1)
                    if isinstance(n, int) and n == 0 and j == 1:
                        take_signs()
                    if isinstance(n, int) and n == 0 and j == NB - 1:
                        channel_scales()

            iterations(dve, step)

        @block.tensor
        def _(pe):
            def hidden(n, b):
                g = n * NB + b
                pe.wait_ge(xn_ready, g + 1)
                if later(g):
                    pe.wait_ge(t_ready, g)
                for t in range(KT):
                    ins = pe.matmul(grid(PS[0:MID, HID, 0:BLK]), W1[:, t, :], XN[:, t, rows_of(b), 1:1 + W],
                                    start=t == 0, stop=t == KT - 1)
                ins.then_inc(hidden_done, 1)

            def weight_tile(g, i, buf):
                if i == 0:
                    pe.wait_ge(t_ready, g + 1)
                if later(g * WT + i):
                    pe.wait_ge(z_ready, g * WT + i)
                pe.matmul(PS[0:TPT * WROWS, WTILE, 0:BLK], W2[:, TPT * i:TPT * (i + 1), :].rearrange("m k r -> m (k r)"),
                          T[:, buf, :], start=True, stop=True).then_inc(tile_done, 1)

            def broadcast(g, buf, k):
                if k % TPT == 0:
                    pe.wait_ge(z_ready, g * WT + k // TPT + 1)
                if later(g * TAPS + k - 1):
                    pe.wait_ge(prod_done, g * TAPS + k - 1)
                r = WROWS * (k % TPT)
                bank = BCAST + 2 * ((buf + k) % 2)
                for t in range(KT):
                    ins = pe.matmul(PS[:, bank + t, 0:BLK], SEL[r:r + WROWS, t, :], WZ[r:r + WROWS, buf, k // TPT, :],
                                    start=True, stop=True)
                ins.then_inc(bcast_done, 1)

            conv_order = [(o, t, k, h) for o in range(KT) for t in range(KT) for k in range(TAPS) for h in range(2)]
            per_tap = len(conv_order) // TAPS

            def convolve(n, b, part):
                for o, t, k, h in conv_order[per_tap * part:per_tap * (part + 1)]:
                    first, last = (t, k, h) == (0, 0, 0), (t, k, h) == (KT - 1, TAPS - 1, 1)
                    if first and o == 0:
                        pe.wait_ge(low_ready, n * NB + min(b + 1, NB - 1) + 1)
                    if first and later((n * NB + b) * KT + o - 1):
                        pe.wait_ge(final_done, (n * NB + b) * KT + o - 1)
                    di, dj = divmod(k, 3)
                    ins = pe.matmul(grid(PS[:, CONV + o, 0:BLK]), CW[:, h, t, k, P * o:P * (o + 1)],
                                    HL[:, h, ROWS * b + di:ROWS * b + di + ROWS, t, dj:dj + W], start=first, stop=last)
                    if last:
                        ins.then_inc(conv_done, 1)

            def group_average(kind, n):
                pe.wait_ge(chain[kind], n * STEPS + 6)
                pe.matmul(PS[:, HID, STAT], GAVG[:, :], AGG[:, kind, :, :].rearrange("p t s -> p (t s)"),
                          start=True, stop=True).then_inc(group_sum[kind], 1)

            pe.wait_ge(consts_loaded, 16 * CONSTS)
            group_average(0, 0)
            pe.wait_ge(consts_ready, 6)
            pe.wait_ge(chain[0], 7)
            hidden(0, 0)
            for i in range(WT):
                weight_tile(0, i, 0)

            def step(im):
                n, parity = im.n, im.parity
                for j in range(NB):
                    nxt = next_block(im, j)
                    for k in range(TAPS):
                        if im.here:
                            broadcast(n * NB + j, (parity + j) % 2, k)
                        c = conv_block(im, j)
                        if c:
                            convolve(c[0], c[2], k)
                        if k == 0 and nxt:
                            if j == 1 and im.before:
                                pe.wait_ge(chain[1], (n - 1) * STEPS + 7)
                            if j == 5 and im.after:
                                pe.wait_ge(chain[0], (n + 1) * STEPS + 7)
                            hidden(nxt[0], nxt[2])
                        if k in (2, 4, 6) and nxt:
                            weight_tile(nxt[0] * NB + nxt[2], k // 2 - 1, (nxt[1] + nxt[2]) % 2)
                        if k == 3 and j == 4 and im.after:
                            pe.wait_ge(t_ready, n * NB + j + 2)
                            group_average(0, n + 1)
                        if k == 7 and j == 0 and im.before:
                            if im.here:
                                pe.wait_ge(t_ready, n * NB + j + 2)
                            group_average(1, n - 1)
                    if isinstance(n, int) and n == 0 and j == 4:
                        pe.wait_ge(abs_ready, 1)
                        wabs = X1[:, 1, :, :].rearrange("p t s -> p (t s)")[:, 0:KT * TAPS * KT * P].rearrange(
                            "p (m o) -> p m o", o=KT * P)
                        for o in range(KT):
                            for m in range(KT * TAPS):
                                ins = pe.matmul(PS[:, CONV + o, 0:1], wabs[:, m, P * o:P * (o + 1)], ONES[:, :],
                                                start=m == 0, stop=m == KT * TAPS - 1)
                            ins.then_inc(abs_summed, 1)

            iterations(pe, step)


def kernel(x, L0_conv_w1, L0_conv_bn_gamma, L0_conv_bn_beta, L0_conv_bn_mean, L0_conv_bn_var, L0_conv_w2,
           L0_conv_b2, L1_conv_weights):
    import numpy as np
    import concourse.bacc as bacc
    from concourse.bass_utils import run_bass_kernel_spmd

    x = np.ascontiguousarray(x)
    B, C = x.shape[:2]
    w1, w2, b2, wc = (np.asarray(a) for a in (L0_conv_w1, L0_conv_w2, L0_conv_b2, L1_conv_weights))
    w2b = np.concatenate([w2.T, b2[None, :]], axis=0).reshape(MID + 1, GROUPS, TAPS).transpose(0, 2, 1)
    sel = np.zeros((TPT, 2, GROUPS, KT, P), np.float16)
    for g in range(GROUPS):
        t, c = divmod(g, GROUPS // KT)
        sel[:, 0, g, t, 16 * c:16 * c + 16] = 1.0
        sel[:, 1, g, t, 16 * c:16 * c + 16] = 1.0 / LOSCALE
    scales = np.zeros((TPT, 2, GROUPS, 2), np.float32)
    scales[:, 0, :, 0], scales[:, 1, :, 0] = 1.0, 1.0 / LOSCALE
    scales[:, 1, :, 1] = -LOSCALE
    arrays = {
        "x_dram": x.reshape(B, C, PIX),
        "w1t_dram": np.ascontiguousarray(w1.T.reshape(KT, P, MID).transpose(1, 0, 2)),
        "bn_dram": np.ascontiguousarray(np.stack([np.asarray(a) for a in (
            L0_conv_bn_gamma, L0_conv_bn_beta, L0_conv_bn_mean, L0_conv_bn_var)], axis=1)),
        "w2t_dram": np.ascontiguousarray(np.concatenate([w2b, w2b], axis=2)),
        "conv_w_dram": np.ascontiguousarray(
            wc.reshape(KT * P, KT, P, TAPS).transpose(2, 1, 3, 0).reshape(P, KT * TAPS * KT * P)),
        "sel_dram": sel.reshape(TPT * WROWS, KT, P),
        "group_avg_dram": np.kron(np.eye(P // 8), np.full((8, 8), 1 / 8)).astype(np.float32),
        "row_scales_dram": scales.reshape(TPT * WROWS, 2),
    }
    nc = bacc.Bacc("TRN2", target_bir_lowering=False, num_devices=1)
    aps = [nc.dram_tensor(k, a.shape, mybir.dt.from_np(a.dtype), kind="ExternalInput").ap() for k, a in arrays.items()]
    out = nc.dram_tensor("out_dram", (B, C, PIX), F32, kind="ExternalOutput").ap()
    program(nc, *aps, out)
    r = run_bass_kernel_spmd(nc, [arrays], core_ids=[0])
    return r.results[0]["out_dram"].reshape(x.shape)
```

```python
from contextlib import ExitStack

import concourse.bass as bass
from concourse import mybir

F32 = mybir.dt.float32
F16 = mybir.dt.float16
ALU = mybir.AluOpType
ACT = mybir.ActivationFunctionType

P = 128
KT = 2
H = W = 56
ROWS = 8
BLK = ROWS * W
NB = H // ROWS
PIX = H * W
HP = H + 2
TAPS = 9
MID = 64
GROUPS = 16
WROWS = 2 * GROUPS
TPT = 3
WT = TAPS // TPT
GN_EPS = 1e-5
BN_EPS = 1e-5
LOSCALE = 2048.0
WSCALE = 32.0
RING = 4
SUMS = TAPS - 1
CONV_LAG = 2
DVE_STEPS = TAPS + 1
PIECES = 8
STEPS = 12


def later(value):
    return not isinstance(value, int) or value > 0


class Image:

    def __init__(self, n, parity, here=True, after=True, before=True, before2=True):
        self.n, self.parity = n, parity
        self.here, self.after, self.before, self.before2 = here, after, before, before2


def program(nc, x, w1t, bn, w2t, b2_rows, conv_w, tap_sel, group_avg, half_scale, low_mask, out):
    B = x.shape[0]
    pairs = (B - 4) // 2
    assert B % 2 == 0 and B >= 4

    def iterations(eng, step):
        def fixed(n):
            step(Image(n, n % 2, n < B, n + 1 < B, 1 <= n <= B, 2 <= n))
        fixed(0)
        fixed(1)
        if pairs > 0:
            with eng.Fori(0, pairs) as i:
                step(Image(i * 2 + 2, 0))
                step(Image(i * 2 + 3, 1))
        for n in range(2 + 2 * max(pairs, 0), B + 2):
            fixed(n)

    x_dram = x.rearrange("b (p t) s -> b p t s", p=P)
    out_dram = out.rearrange("b (p t) s -> b p t s", p=P)

    with ExitStack() as ctx:
        def sb(name, shape, dt=F32):
            return ctx.enter_context(nc.sbuf_tensor(name, shape, dt))

        def sem(name):
            return ctx.enter_context(nc.semaphore(name))

        X = sb("X", [P, 2, KT, PIX])
        X1 = sb("X1", [P, 2, KT, PIX])
        XN = sb("XN", [P, KT, HP, HP])
        HL = sb("HL", [P, 2, HP, KT, HP], F16)
        PROD = sb("PROD", [P, RING, KT, BLK])
        T = sb("T", [P, 2, BLK], F16)
        WH = sb("WH", [TPT * WROWS, 2, BLK], F16)
        WZ = sb("WZ", [TPT * WROWS, 2, WT, BLK], F16)
        CW = sb("CW", [P, 2, KT, TAPS, KT * P], F16)
        W1 = sb("W1", [P, KT, 2 * MID])
        W2F = sb("W2F", [P, TAPS * WROWS])
        W2D = sb("W2D", [P, TAPS * WROWS])
        W2 = sb("W2", [P, 2, TAPS * WROWS], F16)
        B2 = sb("B2", [TPT * WROWS, 3, WT])
        SEL = sb("SEL", [TPT * WROWS, TPT, P], F16)
        GAVG = sb("GAVG", [P, P])
        HSC = sb("HSC", [P, 1])
        MASK = sb("MASK", [TPT * WROWS, 1])
        BN = sb("BN", [P, 4])
        BNF = sb("BNF", [P, 8])
        ONES = sb("ONES", [P, 1])
        CSC = sb("CSC", [P, KT])
        JUNK = [sb("JUNK_X", [P, 2, KT * PIX // PIECES], F16), sb("JUNK_X1", [P, 2, KT * BLK], F16)]
        PART = sb("PART", [P, 2, 2, PIECES])
        TOT = sb("TOT", [P, 2, 2])
        AGG = sb("AGG", [P, 2, 2])
        GRP = sb("GRP", [P, 2, 2])
        MSQ = sb("MSQ", [P, 2])
        DIF = sb("DIF", [P, 2])
        VAR = sb("VAR", [P, 2])
        SD = sb("SD", [P, 2])
        RS0 = sb("RS0", [P, 2])
        TMP = sb("TMP", [P, 2])
        NORM = sb("NORM", [P, 2, 2, 2])
        NORM_LO = sb("NORM_LO", [P, 2, 2])
        PS = ctx.enter_context(nc.psum_tensor("PS", [P, 8, 512], F32))
        HID, WTILE, BCAST, SCR, CONV = 0, 1, 2, 4, 6
        STAT = slice(BLK, BLK + 2)

        x_loaded = [sem(f"x_loaded{t}") for t in range(KT)]
        consts_loaded = sem("consts_loaded")
        convw_loaded = sem("convw_loaded")
        border_ready = sem("border_ready")
        consts_ready = sem("consts_ready")
        bn_sqrt = sem("bn_sqrt")
        signs_ready = sem("signs_ready")
        abs_ready = sem("abs_ready")
        abs_summed = sem("abs_summed")
        chain = [sem("x_chain"), sem("x1_chain")]
        sums_ready = [sem("x_sums_ready"), sem("x1_sums_ready")]
        group_sum = [sem("x_group_sum"), sem("x1_group_sum")]
        sd_ready = [sem("x_sd_ready"), sem("x1_sd_ready")]
        xn_ready = sem("xn_ready")
        hidden_done = sem("hidden_done")
        u_ready = sem("u_ready")
        t_ready = sem("t_ready")
        tile_done = sem("tile_done")
        high_ready = sem("high_ready")
        z_ready = sem("z_ready")
        bcast_done = sem("bcast_done")
        prod_done = sem("prod_done")
        added = sem("added")
        split_ready = sem("split_ready")
        low_ready = sem("low_ready")
        conv_done = sem("conv_done")
        final_done = sem("final_done")
        stored = [sem(f"stored{j}") for j in range(NB)]

        CONSTS = 8
        SETUP = 14

        def rows_of(j):
            return slice(1 + ROWS * j, 1 + ROWS * (j + 1))

        def cols_of(j):
            return slice(BLK * j, BLK * (j + 1))

        def grid(ap):
            return ap.rearrange("p (r c) -> p r c", c=W)

        def conv_block(im, j):
            if j >= CONV_LAG:
                return (im.n - 1, 1 - im.parity, j - CONV_LAG) if im.before else None
            return (im.n - 2, im.parity, j + NB - CONV_LAG) if im.before2 else None

        def last_conv_block(im, j):
            if j >= 1:
                return conv_block(im, j - 1)
            return (im.n - 2, im.parity, NB - 1 - CONV_LAG) if im.before2 else None

        def next_block(im, j):
            if j + 1 < NB:
                return (im.n, im.parity, j + 1) if im.here else None
            return (im.n + 1, 1 - im.parity, 0) if im.after else None

        def norm_block(im, j):
            if j < NB - 2:
                return (im.n, im.parity, j + 2) if im.here else None
            return (im.n + 1, 1 - im.parity, j - (NB - 2)) if im.after else None

        block = ctx.enter_context(nc.Block())

        @block.sync
        def _(sp):
            def load_image(n, parity):
                for t in range(KT):
                    src = x_dram[n] if isinstance(n, int) else x_dram[bass.ds(n, 1)].rearrange("a p t s -> (a p) t s")
                    sp.dma_start(X[:, parity, t, :], src[:, t, :]).then_inc(x_loaded[t], 16)

            load_image(0, 0)
            for dst, src in ((GAVG[:, :], group_avg), (W1[:, :, :], w1t), (BN[:, :], bn), (W2F[:, :], w2t),
                             (B2[:, 0, :], b2_rows), (SEL[:, :, :], tap_sel), (HSC[:, :], half_scale), (MASK[:, :], low_mask)):
                sp.dma_start(dst, src).then_inc(consts_loaded, 16)
            sp.dma_start(X1[:, 1, :, :].rearrange("p t s -> p (t s)")[:, 0:KT * TAPS * KT * P], conv_w
                         ).then_inc(convw_loaded, 16)

            def step(im):
                for j in range(NB):
                    c = last_conv_block(im, j)
                    if c:
                        n, parity, b = c
                        if later(n):
                            sp.wait_ge(stored[b], n * 16)
                        sp.wait_ge(final_done, (n * NB + b + 1) * KT)
                        dst = out_dram[n] if isinstance(n, int) else out_dram[bass.ds(n, 1)].rearrange("a p t s -> (a p) t s")
                        sp.dma_start(dst[:, :, cols_of(b)], X1[:, parity, :, cols_of(b)]).then_inc(stored[b], 16)
                    if j == 0 and im.after:
                        if later(im.n):
                            sp.wait_ge(added, im.n * (NB * SUMS))
                        sp.wait_ge(sums_ready[0], (im.n + 1) * PIECES * 2)
                        load_image(im.n + 1, 1 - im.parity)

            iterations(sp, step)
            for b in range(NB):
                sp.wait_ge(stored[b], 16 * B)

        @block.gpsimd
        def _(pool):
            pool.memset(HL[:, :, :, :, :].rearrange("p h r t c -> p (h r t c)").bitcast(F32), 0.0).then_inc(border_ready, 1)

            def step(im):
                if not im.here:
                    return
                n, parity = im.n, im.parity
                for j in range(NB):
                    for k in range(SUMS):
                        done = (n * NB + j) * SUMS + k
                        if k == 0:
                            if later(n - 1):
                                pool.wait_ge(stored[j], (n - 1) * 16)
                            if isinstance(n, int) and n == 1 and j == 0:
                                pool.wait_ge(abs_summed, 2)
                        if later(done):
                            pool.wait_ge(added, done)
                        pool.wait_ge(prod_done, (n * NB + j) * DVE_STEPS + (k + 1 if k < SUMS - 1 else DVE_STEPS))
                        acc = X1[:, parity, :, cols_of(j)]
                        before = X[:, parity, :, cols_of(j)] if k == 0 else acc
                        pool.tensor_tensor(acc, before, PROD[:, k % RING, :, :], ALU.add).then_inc(added, 1)

            iterations(pool, step)

        @block.scalar
        def _(act):
            def piece_sums(kind, src, piece, before):
                for h, func in enumerate((ACT.Identity, ACT.Square)):
                    junk = JUNK[kind][:, h, :].rearrange("p (a b) -> p a b", b=src.shape[2])
                    if later(before + h - 1):
                        act.wait_ge(sums_ready[kind], before + h - 1)
                    act.activation(junk, src, func, accum_out=PART[:, kind, h, piece:piece + 1]
                                   ).then_inc(sums_ready[kind], 1)

            def x_piece(n, parity, piece):
                t, quarter = divmod(piece, PIECES // KT)
                if quarter == 0:
                    act.wait_ge(x_loaded[t], (n + 1) * 16)
                size = KT * PIX // PIECES
                src = X[:, parity, t, quarter * size:(quarter + 1) * size].rearrange("p (a b) -> p a b", a=2)
                piece_sums(0, src, piece, (n * PIECES + piece) * 2)

            def x1_piece(n, parity, b):
                act.wait_ge(added, (n * NB + b + 1) * SUMS)
                if b == 0 and later(n):
                    act.wait_ge(chain[1], (n - 1) * STEPS + 1)
                piece_sums(1, X1[:, parity, :, cols_of(b)], b, (n * NB + b) * 2)

            def normalise(n, parity, b):
                if b == 0 or (b == 1 and isinstance(n, int) and n == 0):
                    act.wait_ge(chain[0], (n + 1) * STEPS)
                last_reader = (n - 1) * NB + min(b + 1, NB - 1) + 1
                if later(last_reader):
                    act.wait_ge(prod_done, last_reader * DVE_STEPS)
                act.activation(XN[:, :, rows_of(b), 1:1 + W],
                               X[:, parity, :, cols_of(b)].rearrange("p t (r c) -> p t r c", c=W), ACT.Identity,
                               bias=NORM[:, 0, parity, 1:2], scale=NORM[:, 0, parity, 0:1]).then_inc(xn_ready, 1)

            def hidden(g, buf):
                act.wait_ge(hidden_done, g + 1)
                if later(g - 1):
                    act.wait_ge(tile_done, (g - 1) * WT)
                act.activation(T[:, buf, :], PS[:, HID, 0:BLK], ACT.Relu, bias=BNF[:, 5:6], scale=BNF[:, 3:4]
                               ).then_inc(u_ready, 1)
                low = PS[MID:P, HID, 0:BLK]
                act.wait_ge(u_ready, 2 * g + 1)
                act.activation(low, low, ACT.Relu, bias=BNF[MID:P, 7:8], scale=BNF[MID:P, 6:7]).then_inc(u_ready, 1)

            def high(g, i, buf):
                act.wait_ge(tile_done, g * WT + i + 1)
                if later(g * WT + i - 1):
                    act.wait_ge(z_ready, g * WT + i - 1)
                act.activation(WH[:, buf, :], PS[0:TPT * WROWS, WTILE, 0:BLK], ACT.Identity,
                               bias=B2[:, 2, i:i + 1], scale=MASK[:, :]).then_inc(high_ready, 1)

            def split(n, parity, b, slot):
                if b == 0:
                    act.wait_ge(chain[1], (n + 1) * STEPS)
                g = n * NB + b
                if later(g):
                    act.wait_ge(low_ready, g)
                act.wait_ge(prod_done, slot * DVE_STEPS)
                last_reader = (n - 1) * NB + min(b + 1, NB - 1) + 1
                if later(last_reader):
                    act.wait_ge(conv_done, last_reader * KT)
                src = X1[:, parity, :, cols_of(b)]
                act.activation(PS[:, SCR:SCR + KT, 0:BLK], src, ACT.Identity, bias=NORM_LO[:, parity, 1:2],
                               scale=NORM_LO[:, parity, 0:1])
                act.activation(HL[:, 0, rows_of(b), :, 1:1 + W].rearrange("p r t c -> p t r c"),
                               src.rearrange("p t (r c) -> p t r c", c=W), ACT.Identity,
                               bias=NORM[:, 1, parity, 1:2], scale=NORM[:, 1, parity, 0:1]).then_inc(split_ready, 1)

            def root(kind, n):
                act.wait_ge(chain[kind], n * STEPS + 6)
                act.activation(SD[:, kind:kind + 1], VAR[:, kind:kind + 1], ACT.Sqrt).then_inc(sd_ready[kind], 1)

            for piece in range(PIECES):
                x_piece(0, 0, piece)
            act.wait_ge(consts_ready, 1)
            act.activation(BNF[:, 1:2], BNF[:, 0:1], ACT.Sqrt).then_inc(bn_sqrt, 1)
            root(0, 0)
            act.wait_ge(border_ready, 3)
            normalise(0, 0, 0)
            normalise(0, 0, 1)
            act.wait_ge(consts_ready, SETUP)
            hidden(0, 0)
            for i in range(WT - 1):
                high(0, i, i % 2)

            def step(im):
                for j in range(NB):
                    nxt = next_block(im, j)
                    slot = min(im.n * NB + j, B * NB) if isinstance(im.n, int) else im.n * NB + j
                    if im.before and j >= 2:
                        split(im.n - 1, 1 - im.parity, j, slot)
                    if im.here:
                        high(im.n * NB + j, 2, (im.parity + j) % 2)
                    if nxt:
                        n, parity, b = nxt
                        g, buf = n * NB + b, (parity + b) % 2
                        hidden(g, buf)
                    if im.before and j == 1:
                        split(im.n - 1, 1 - im.parity, 0, slot)
                    if norm_block(im, j):
                        normalise(*norm_block(im, j))
                    if im.before and j == 1:
                        split(im.n - 1, 1 - im.parity, 1, slot)
                    if nxt:
                        high(g, 0, buf)
                    if j >= 1 and im.here:
                        x1_piece(im.n, im.parity, j - 1)
                    if j == 0 and im.before:
                        x1_piece(im.n - 1, 1 - im.parity, NB - 1)
                    if 1 <= j <= 3 and im.after:
                        for piece in ((0, 1), (2, 3, 4), (5, 6, 7))[j - 1]:
                            x_piece(im.n + 1, 1 - im.parity, piece)
                    if nxt:
                        high(g, 1, (buf + 1) % 2)
                    if j == 0 and im.before:
                        root(1, im.n - 1)
                    if j == 4 and im.after:
                        root(0, im.n + 1)
                    if j == 3 and isinstance(im.n, int) and im.n == 0:
                        act.wait_ge(signs_ready, 2)
                        wraw = X1[:, 1, :, :].rearrange("p t s -> p (t s)")[:, 0:KT * TAPS * KT * P]
                        act.activation(wraw, wraw, ACT.Abs).then_inc(abs_ready, 1)

            iterations(act, step)

        @block.vector
        def _(dve):
            def link(ins, kind, value):
                ins.then_inc(chain[kind], 1)
                dve.wait_ge(chain[kind], value)

            def channel_stats(kind, n):
                pieces = PIECES if kind == 0 else NB
                dve.wait_ge(sums_ready[kind], (n + 1) * pieces * 2)
                link(dve.tensor_reduce(TOT[:, kind, :], PART[:, kind, :, 0:pieces], mybir.AxisListType.X, ALU.add),
                     kind, n * STEPS + 1)
                dve.tensor_scalar(AGG[:, kind, :], TOT[:, kind, :], 1.0 / (KT * PIX), None, ALU.mult
                                  ).then_inc(chain[kind], 1)

            def group_variance(kind, n):
                s = n * STEPS
                one = slice(kind, kind + 1)
                dve.wait_ge(group_sum[kind], n + 1)
                link(dve.tensor_copy(GRP[:, kind, :], PS[:, HID, STAT]), kind, s + 3)
                link(dve.tensor_tensor(MSQ[:, one], GRP[:, kind, 0:1], GRP[:, kind, 0:1], ALU.mult), kind, s + 4)
                link(dve.tensor_tensor(DIF[:, one], GRP[:, kind, 1:2], MSQ[:, one], ALU.subtract), kind, s + 5)
                dve.tensor_scalar(VAR[:, one], DIF[:, one], 0.0, GN_EPS, ALU.max, ALU.add).then_inc(chain[kind], 1)

            def scale_and_bias(kind, n, parity):
                s = n * STEPS
                one = slice(kind, kind + 1)
                scale, bias = NORM[:, kind, parity, 0:1], NORM[:, kind, parity, 1:2]
                dve.wait_ge(sd_ready[kind], n + 1)
                link(dve.reciprocal(RS0[:, one], SD[:, one]), kind, s + 7)
                link(dve.scalar_tensor_tensor(out=TMP[:, one], in0=RS0[:, one], scalar=RS0[:, one], in1=VAR[:, one],
                                              op0=ALU.mult, op1=ALU.mult), kind, s + 8)
                link(dve.tensor_scalar(MSQ[:, one], TMP[:, one], -0.5, 1.5, ALU.mult, ALU.add), kind, s + 9)
                link(dve.tensor_tensor(scale, RS0[:, one], MSQ[:, one], ALU.mult), kind, s + 10)
                link(dve.scalar_tensor_tensor(out=bias, in0=GRP[:, kind, 0:1], scalar=-1.0, in1=scale,
                                              op0=ALU.mult, op1=ALU.mult), kind, s + 11)
                dve.tensor_scalar(NORM_LO[:, parity, :] if kind == 1 else TOT[:, 0, :], NORM[:, kind, parity, :], LOSCALE,
                                  None, ALU.mult).then_inc(chain[kind], 1)

            def ring(g, k):
                if later(g * SUMS + k + 1 - RING):
                    dve.wait_ge(added, g * SUMS + k + 1 - RING)

            def product(g, parity, j, k):
                dve.wait_ge(bcast_done, g * TAPS + k + 1)
                di, dj = divmod(k, 3)
                shifted = XN[:, :, ROWS * j + di:ROWS * j + di + ROWS, dj:dj + W]
                weights = PS[:, BCAST + (parity + j + k) % 2, 0:BLK].rearrange(
                    "p (t r c) -> p t r c", t=1, c=W).to_broadcast([P, KT, ROWS, W])
                if k < TAPS - 1:
                    dst = PROD[:, k % RING, :, :]
                else:
                    dst = PS[:, SCR:SCR + KT, 0:BLK]
                dve.tensor_tensor(dst.rearrange("p t (r c) -> p t r c", c=W), weights, shifted, ALU.mult
                                         ).then_inc(prod_done, 1)

            def low_activations(g, buf):
                dve.wait_ge(u_ready, 2 * g + 2)
                low = T[MID:P, buf, :]
                dve.scalar_tensor_tensor(out=low, in0=low, scalar=-LOSCALE, in1=PS[MID:P, HID, 0:BLK],
                                         op0=ALU.mult, op1=ALU.add).then_inc(t_ready, 1)

            def low_rows(g, i, buf):
                dve.wait_ge(high_ready, g * WT + i + 1)
                dve.scalar_tensor_tensor(out=WZ[:, buf, i, :], in0=PS[0:TPT * WROWS, WTILE, 0:BLK], scalar=B2[:, 1, i:i + 1],
                                         in1=WH[:, (buf + i) % 2, :], op0=ALU.add, op1=ALU.subtract).then_inc(z_ready, 1)

            def low_half(n, b):
                dve.wait_ge(split_ready, n * NB + b + 1)
                for t in range(KT):
                    ins = dve.scalar_tensor_tensor(out=HL[:, 1, rows_of(b), t, 1:1 + W], in0=HL[:, 0, rows_of(b), t, 1:1 + W],
                                                   scalar=-LOSCALE, in1=grid(PS[:, SCR + t, 0:BLK]), op0=ALU.mult, op1=ALU.add)
                ins.then_inc(low_ready, 1)

            def residual(n, parity, b, t):
                dve.wait_ge(conv_done, (n * NB + b) * KT + t + 1)
                o = X1[:, parity, t, cols_of(b)]
                dve.scalar_tensor_tensor(out=o, in0=PS[:, CONV + t, 0:BLK], scalar=CSC[:, t:t + 1], in1=o,
                                         op0=ALU.mult, op1=ALU.add).then_inc(final_done, 1)

            def setup(ins, value=None):
                ins.then_inc(consts_ready, 1)
                if value:
                    dve.wait_ge(consts_ready, value)

            dve.memset(XN[:, :, :, :], 0.0).then_inc(border_ready, 1)
            dve.memset(ONES[:, :], 1.0).then_inc(border_ready, 1)
            dve.wait_ge(consts_loaded, 16 * CONSTS)
            setup(dve.tensor_scalar(BNF[:, 0:1], BN[:, 3:4], BN_EPS, None, ALU.add))
            setup(dve.tensor_scalar(W2F[:, :], W2F[:, :], WSCALE, None, ALU.mult), 2)
            setup(dve.tensor_copy(W2[:, 0, :], W2F[:, :]), 3)
            setup(dve.tensor_tensor(W2D[:, :], W2F[:, :], W2[:, 0, :], ALU.subtract), 4)
            setup(dve.tensor_scalar(W2[:, 1, :], W2D[:, :], HSC[:, :], None, ALU.mult))
            setup(dve.tensor_scalar(W2[:, 0, :], W2[:, 0, :], HSC[:, :], None, ALU.mult))
            setup(dve.tensor_scalar(B2[:, 1, :], B2[:, 0, :], WSCALE, None, ALU.mult), 7)
            setup(dve.tensor_scalar(B2[:, 2, :], B2[:, 1, :], MASK[:, :], None, ALU.mult))
            channel_stats(0, 0)
            dve.wait_ge(bn_sqrt, 1)
            setup(dve.reciprocal(BNF[:, 2:3], BNF[:, 1:2]), 9)
            setup(dve.tensor_tensor(BNF[:, 3:4], BN[:, 0:1], BNF[:, 2:3], ALU.mult), 10)
            setup(dve.tensor_tensor(BNF[:, 4:5], BN[:, 2:3], BNF[:, 3:4], ALU.mult), 11)
            setup(dve.tensor_tensor(BNF[:, 5:6], BN[:, 1:2], BNF[:, 4:5], ALU.subtract), 12)
            setup(dve.tensor_scalar(BNF[:, 6:7], BNF[:, 3:4], LOSCALE, None, ALU.mult))
            setup(dve.tensor_scalar(BNF[:, 7:8], BNF[:, 5:6], LOSCALE, None, ALU.mult))
            group_variance(0, 0)
            scale_and_bias(0, 0, 0)
            low_activations(0, 0)
            for i in range(WT - 1):
                low_rows(0, i, 0)

            def take_signs():
                dve.wait_ge(convw_loaded, 16)
                wraw = X1[:, 1, :, :].rearrange("p t s -> p (t s)")[:, 0:KT * TAPS * KT * P]
                hi = CW[:, 0, :, :, :].rearrange("p t k o -> p (t k o)")
                lo = CW[:, 1, :, :, :].rearrange("p t k o -> p (t k o)")
                dve.tensor_scalar(hi, wraw, 0.0, None, ALU.is_lt).then_inc(signs_ready, 1)
                dve.wait_ge(signs_ready, 1)
                dve.scalar_tensor_tensor(out=hi, in0=wraw, scalar=0.0, in1=hi, op0=ALU.is_gt,
                                         op1=ALU.subtract).then_inc(signs_ready, 1)
                dve.wait_ge(signs_ready, 2)
                dve.tensor_scalar(lo, hi, 1.0 / LOSCALE, None, ALU.mult).then_inc(signs_ready, 1)

            def channel_scales():
                dve.wait_ge(abs_summed, 2)
                for t in range(KT):
                    ins = dve.tensor_scalar(CSC[:, t:t + 1], PS[:, CONV + t, 0:1], 1.0 / (KT * P * TAPS), None, ALU.mult)
                ins.then_inc(signs_ready, 1)

            def step(im):
                n, parity = im.n, im.parity
                for j in range(NB):
                    nxt = next_block(im, j)
                    if nxt:
                        next_g, buf = nxt[0] * NB + nxt[2], (nxt[1] + nxt[2]) % 2
                    for k in range(TAPS):
                        if im.here:
                            g = n * NB + j
                            if k == 0:
                                dve.wait_ge(xn_ready, n * NB + min(j + 1, NB - 1) + 1)
                            if k < TAPS - 1:
                                ring(g, k)
                            split_so_far = (n - 1) * NB + (j + 1 if j else 0)
                            if k == TAPS - 1 and later(split_so_far):
                                dve.wait_ge(low_ready, split_so_far)
                            product(g, parity, j, k)
                        if k == 0 and j == 1 and im.before:
                            scale_and_bias(1, n - 1, 1 - parity)
                        if k == 0 and last_conv_block(im, j):
                            residual(*last_conv_block(im, j), 1)
                        if k == 1 and j >= 2 and im.before:
                            low_half(n - 1, j)
                        if k == 2 and im.here:
                            low_rows(g, 2, (parity + j) % 2)
                        if k == 2 and nxt:
                            low_activations(next_g, buf)
                        if k == 2 and j == 4 and im.after:
                            channel_stats(0, n + 1)
                        if k == 3 and j == 1 and im.before:
                            low_half(n - 1, 0)
                        if k == 5 and nxt:
                            low_rows(next_g, 0, buf)
                        if k == 5 and conv_block(im, j):
                            residual(*conv_block(im, j), 0)
                        if k == 6 and j == 1 and im.before:
                            low_half(n - 1, 1)
                        if k == 6 and j == 4 and im.after:
                            group_variance(0, n + 1)
                        if k == 6 and j == 0 and im.before:
                            channel_stats(1, n - 1)
                        if k == 8 and nxt:
                            low_rows(next_g, 1, buf)
                        if k == 8 and j == 0 and im.before:
                            group_variance(1, n - 1)
                        if k == 8 and im.here:
                            dve.wait_ge(prod_done, g * DVE_STEPS + TAPS)
                            dst = PROD[:, (TAPS - 2) % RING, :, :]
                            dve.tensor_tensor(dst, PS[:, SCR:SCR + KT, 0:BLK], dst, ALU.add).then_inc(prod_done, 1)
                        if k == 8 and j == 4 and im.after:
                            scale_and_bias(0, n + 1, 1 - parity)
                    if isinstance(n, int) and n == 0 and j == 1:
                        take_signs()
                    if isinstance(n, int) and n == 0 and j == NB - 1:
                        channel_scales()

            iterations(dve, step)

        @block.tensor
        def _(pe):
            def hidden(n, b):
                g = n * NB + b
                pe.wait_ge(xn_ready, g + 1)
                if later(g):
                    pe.wait_ge(t_ready, g)
                for t in range(KT):
                    ins = pe.matmul(grid(PS[:, HID, 0:BLK]), W1[:, t, :], XN[:, t, rows_of(b), 1:1 + W],
                                    start=t == 0, stop=t == KT - 1)
                ins.then_inc(hidden_done, 1)

            def weight_tile(g, i, buf):
                if i == 0:
                    pe.wait_ge(t_ready, g + 1)
                if later(g * WT + i):
                    pe.wait_ge(z_ready, g * WT + i)
                for h in range(2):
                    ins = pe.matmul(PS[0:TPT * WROWS, WTILE, 0:BLK], W2[:, h, TPT * WROWS * i:TPT * WROWS * (i + 1)],
                                    T[:, buf, :], start=h == 0, stop=h == 1)
                ins.then_inc(tile_done, 1)

            def broadcast(g, buf, k):
                if k % TPT == 0:
                    pe.wait_ge(z_ready, g * WT + k // TPT + 1)
                last_use = g * DVE_STEPS + (k - 1 if k >= 2 else k - 2)
                if later(last_use):
                    pe.wait_ge(prod_done, last_use)
                pe.matmul(PS[:, BCAST + (buf + k) % 2, 0:BLK], SEL[:, k % TPT, :], WZ[:, buf, k // TPT, :],
                          start=True, stop=True).then_inc(bcast_done, 1)

            conv_order = [(o, t, k, h) for o in range(KT) for t in range(KT) for k in range(TAPS) for h in range(2)]
            per_tap = len(conv_order) // TAPS

            def convolve(n, b, part):
                for o, t, k, h in conv_order[per_tap * part:per_tap * (part + 1)]:
                    first, last = (t, k, h) == (0, 0, 0), (t, k, h) == (KT - 1, TAPS - 1, 1)
                    if first and o == 0:
                        pe.wait_ge(low_ready, n * NB + min(b + 1, NB - 1) + 1)
                    if first and later((n * NB + b) * KT + o - 1):
                        pe.wait_ge(final_done, (n * NB + b) * KT + o - 1)
                    di, dj = divmod(k, 3)
                    ins = pe.matmul(grid(PS[:, CONV + o, 0:BLK]), CW[:, h, t, k, P * o:P * (o + 1)],
                                    HL[:, h, ROWS * b + di:ROWS * b + di + ROWS, t, dj:dj + W], start=first, stop=last)
                    if last:
                        ins.then_inc(conv_done, 1)

            def group_average(kind, n):
                pe.wait_ge(chain[kind], n * STEPS + 2)
                pe.matmul(PS[:, HID, STAT], GAVG[:, :], AGG[:, kind, :], start=True, stop=True).then_inc(group_sum[kind], 1)

            pe.wait_ge(consts_loaded, 16 * CONSTS)
            group_average(0, 0)
            pe.wait_ge(consts_ready, SETUP)
            pe.wait_ge(chain[0], 3)
            hidden(0, 0)
            for i in range(WT - 1):
                weight_tile(0, i, 0)

            def step(im):
                n, parity = im.n, im.parity
                for j in range(NB):
                    nxt = next_block(im, j)
                    for k in range(TAPS):
                        if im.here:
                            broadcast(n * NB + j, (parity + j) % 2, k)
                        c = conv_block(im, j)
                        if c:
                            convolve(c[0], c[2], k)
                        if k == 0 and im.here:
                            weight_tile(n * NB + j, 2, (parity + j) % 2)
                        if k == 0 and nxt:
                            if j == 1 and im.before:
                                pe.wait_ge(chain[1], (n - 1) * STEPS + 3)
                            if j == 5 and im.after:
                                pe.wait_ge(chain[0], (n + 1) * STEPS + 3)
                            hidden(nxt[0], nxt[2])
                        if k in (3, 6) and nxt:
                            weight_tile(nxt[0] * NB + nxt[2], k // 3 - 1, (nxt[1] + nxt[2]) % 2)
                        if k == 4 and j == 4 and im.after:
                            pe.wait_ge(t_ready, n * NB + j + 2)
                            group_average(0, n + 1)
                        if k == 7 and j == 0 and im.before:
                            if im.here:
                                pe.wait_ge(t_ready, n * NB + j + 2)
                            group_average(1, n - 1)
                    if isinstance(n, int) and n == 0 and j == 4:
                        pe.wait_ge(abs_ready, 1)
                        wabs = X1[:, 1, :, :].rearrange("p t s -> p (t s)")[:, 0:KT * TAPS * KT * P].rearrange(
                            "p (m o) -> p m o", o=KT * P)
                        for o in range(KT):
                            for m in range(KT * TAPS):
                                ins = pe.matmul(PS[:, CONV + o, 0:1], wabs[:, m, P * o:P * (o + 1)], ONES[:, :],
                                                start=m == 0, stop=m == KT * TAPS - 1)
                            ins.then_inc(abs_summed, 1)

            iterations(pe, step)


def kernel(x, L0_conv_w1, L0_conv_bn_gamma, L0_conv_bn_beta, L0_conv_bn_mean, L0_conv_bn_var, L0_conv_w2,
           L0_conv_b2, L1_conv_weights):
    import numpy as np
    import concourse.bacc as bacc
    from concourse.bass_utils import run_bass_kernel_spmd

    x = np.ascontiguousarray(x)
    B, C = x.shape[:2]
    w1, w2, b2, wc = (np.asarray(a) for a in (L0_conv_w1, L0_conv_w2, L0_conv_b2, L1_conv_weights))
    w2k = w2.T.reshape(MID, GROUPS, TAPS).transpose(0, 2, 1)
    w2k = np.stack([w2k, w2k], axis=2).reshape(MID, TAPS * WROWS)
    b2k = b2.reshape(GROUPS, TAPS).T
    b2k = np.stack([b2k, b2k], axis=1).reshape(WT, TPT * WROWS).T
    w1t = w1.T.reshape(P, KT, MID)
    bn = np.stack([np.asarray(a) for a in (L0_conv_bn_gamma, L0_conv_bn_beta, L0_conv_bn_mean, L0_conv_bn_var)], axis=1)
    sel = np.zeros((TPT, 2, GROUPS, TPT, P), np.float16)
    for k in range(TPT):
        for g in range(GROUPS):
            sel[k, :, g, k, P // GROUPS * g:P // GROUPS * (g + 1)] = 1.0 / WSCALE
    half_scale = np.repeat(np.float32([1.0, 1.0 / LOSCALE]), MID)[:, None]
    low_mask = np.tile(np.repeat(np.float32([0.0, 1.0]), GROUPS), TPT)[:, None]
    arrays = {
        "x_dram": x.reshape(B, C, PIX),
        "w1t_dram": np.ascontiguousarray(np.concatenate([w1t, w1t], axis=2)),
        "bn_dram": np.ascontiguousarray(np.concatenate([bn, bn], axis=0)),
        "w2t_dram": np.ascontiguousarray(np.concatenate([w2k, w2k], axis=0)),
        "b2_dram": np.ascontiguousarray(b2k),
        "conv_w_dram": np.ascontiguousarray(
            wc.reshape(P, KT, P, KT, TAPS).transpose(2, 3, 4, 1, 0).reshape(P, KT * TAPS * KT * P)),
        "sel_dram": sel.reshape(TPT * WROWS, TPT, P),
        "group_avg_dram": np.kron(np.eye(P // 4), np.full((4, 4), 1 / 4)).astype(np.float32),
        "half_scale_dram": np.ascontiguousarray(half_scale),
        "low_mask_dram": np.ascontiguousarray(low_mask),
    }
    nc = bacc.Bacc("TRN2", target_bir_lowering=False, num_devices=1)
    aps = [nc.dram_tensor(k, a.shape, mybir.dt.from_np(a.dtype), kind="ExternalInput").ap() for k, a in arrays.items()]
    out = nc.dram_tensor("out_dram", (B, C, PIX), F32, kind="ExternalOutput").ap()
    program(nc, *aps, out)
    r = run_bass_kernel_spmd(nc, [arrays], core_ids=[0])
    return r.results[0]["out_dram"].reshape(x.shape)
```

```python
from contextlib import ExitStack

import concourse.bass as bass
from concourse import mybir

F32 = mybir.dt.float32
F16 = mybir.dt.float16
ALU = mybir.AluOpType
ACT = mybir.ActivationFunctionType

P = 128
KT = 2
H = W = 56
ROWS = 8
BLK = ROWS * W
NB = H // ROWS
PIX = H * W
HP = H + 2
TAPS = 9
MID = 64
GROUPS = 16
WROWS = 2 * GROUPS
TPT = 3
WT = TAPS // TPT
GN_EPS = 1e-5
BN_EPS = 1e-5
LOSCALE = 2048.0
WSCALE = 32.0
XSCALE = 256.0
W1SCALE = 64.0
RING = 4
SUMS = TAPS - 1
CONV_LAG = 2
PIECES = 8
STEPS = 12


def later(value):
    return not isinstance(value, int) or value > 0


class Image:

    def __init__(self, n, parity, here=True, after=True, before=True, before2=True, after2=True):
        self.n, self.parity = n, parity
        self.here, self.after, self.after2, self.before, self.before2 = here, after, after2, before, before2


def program(nc, x, w1t, bn, w2t, b2_rows, conv_w, tap_sel, group_avg, identity, half_scale, low_mask, out):
    B = x.shape[0]
    pairs = (B - 4) // 2
    assert B % 2 == 0 and B >= 4

    def iterations(eng, step):
        def fixed(n):
            step(Image(n, n % 2, n < B, n + 1 < B, 1 <= n <= B, 2 <= n, n + 2 < B))
        fixed(0)
        fixed(1)
        if pairs > 0:
            with eng.Fori(0, pairs) as i:
                step(Image(i * 2 + 2, 0))
                step(Image(i * 2 + 3, 1))
        for n in range(2 + 2 * max(pairs, 0), B + 2):
            fixed(n)

    x_dram = x.rearrange("b (p t) s -> b p t s", p=P)
    out_dram = out.rearrange("b (p t) s -> b p t s", p=P)

    with ExitStack() as ctx:
        def sb(name, shape, dt=F32):
            return ctx.enter_context(nc.sbuf_tensor(name, shape, dt))

        def sem(name):
            return ctx.enter_context(nc.semaphore(name))

        X = sb("X", [P, 2, KT, PIX])
        X1 = sb("X1", [P, 2, KT, PIX])
        XN = sb("XN", [P, KT, HP, HP])
        HL = sb("HL", [P, 2, HP, KT, HP], F16)
        PROD = sb("PROD", [P, RING, KT, BLK])
        T = sb("T", [P, 2, BLK], F16)
        WH = sb("WH", [TPT * WROWS, 2, BLK], F16)
        WZ = sb("WZ", [TPT * WROWS, 2, WT, BLK], F16)
        CW = sb("CW", [P, 2, KT, TAPS, KT * P], F16)
        XS = sb("XS", [P, 2, KT, BLK], F16)
        W1 = sb("W1", [P, 2, KT, 2 * MID], F16)
        W2F = sb("W2F", [P, TAPS * WROWS])
        W2D = sb("W2D", [P, TAPS * WROWS])
        W2 = sb("W2", [P, 2, TAPS * WROWS], F16)
        B2 = sb("B2", [TPT * WROWS, 3, WT])
        SEL = sb("SEL", [TPT * WROWS, TPT, P], F16)
        GAVG = sb("GAVG", [P, P])
        HSC = sb("HSC", [P, 1])
        MASK = sb("MASK", [TPT * WROWS, 1])
        BN = sb("BN", [P, 4])
        BNF = sb("BNF", [P, 9])
        ONES = sb("ONES", [P, 1])
        CSC = sb("CSC", [P, KT])
        JUNK = [sb("JUNK_X", [P, 2, KT * PIX // PIECES], F16), sb("JUNK_X1", [P, 2, KT * BLK], F16)]
        PART = sb("PART", [P, 2, 2, PIECES])
        TOT = sb("TOT", [P, 2, 2])
        AGG = sb("AGG", [P, 2, 2])
        GRP = sb("GRP", [P, 2, 2])
        MSQ = sb("MSQ", [P, 2])
        DIF = sb("DIF", [P, 2])
        VAR = sb("VAR", [P, 2])
        SD = sb("SD", [P, 2])
        RS0 = sb("RS0", [P, 2])
        TMP = sb("TMP", [P, 2])
        NORM = sb("NORM", [P, 2, 2, 2])
        NORM_UP = sb("NORM_UP", [P, 2, 2, 2])
        BACK = sb("BACK", [P, 2, 2])
        PS = ctx.enter_context(nc.psum_tensor("PS", [P, 8, 512], F32))
        HID, WTILE, BCAST, SCR, CONV = 0, 1, 2, 4, 6
        STAT = slice(BLK, BLK + 2)

        x_loaded = [sem(f"x_loaded{t}") for t in range(KT)]
        first_loaded = [sem(f"first_loaded{i}") for i in range(2 * KT)]
        consts_loaded = sem("consts_loaded")
        convw_loaded = sem("convw_loaded")
        ones_ready = sem("ones_ready")
        border_ready = sem("border_ready")
        consts_ready = sem("consts_ready")
        bn_sqrt = sem("bn_sqrt")
        signs_ready = sem("signs_ready")
        scales_ready = sem("scales_ready")
        abs_ready = sem("abs_ready")
        abs_added = sem("abs_added")
        abs_summed = sem("abs_summed")
        chain = [sem("x_chain"), sem("x1_chain")]
        sums_ready = [sem("x_sums_ready"), sem("x1_sums_ready")]
        squares_ready = sem("squares_ready")
        tensor_added = sem("tensor_added")
        group_sum = [sem("x_group_sum"), sem("x1_group_sum")]
        sd_ready = [sem("x_sd_ready"), sem("x1_sd_ready")]
        xn_ready = sem("xn_ready")
        xh_ready = sem("xh_ready")
        xl_ready = sem("xl_ready")
        hidden_done = sem("hidden_done")
        u_ready = sem("u_ready")
        t_ready = sem("t_ready")
        tile_done = sem("tile_done")
        high_ready = sem("high_ready")
        z_ready = sem("z_ready")
        bcast_done = sem("bcast_done")
        prod_done = sem("prod_done")
        last_ready = sem("last_ready")
        added = sem("added")
        split_ready = sem("split_ready")
        low_ready = sem("low_ready")
        conv_done = sem("conv_done")
        final_done = sem("final_done")
        stored = [sem(f"stored{j}") for j in range(NB)]

        CONSTS = 9
        W1_SETUP, BN_SETUP, SETUP = 4, 11, 18

        spare = X1[:, 1, :, :].rearrange("p t s -> p (t s)")
        WRAW = spare[:, 0:KT * TAPS * KT * P]
        IDENT = spare[:, KT * TAPS * KT * P:KT * TAPS * KT * P + P]
        LAST = spare[:, KT * TAPS * KT * P + P:KT * TAPS * KT * P + P + KT * BLK].rearrange("p (t s) -> p t s", t=KT)
        W1F = spare[:, KT * TAPS * KT * P + P + KT * BLK:][:, 0:KT * 2 * MID].rearrange("p (t m) -> p t m", t=KT)
        TENSOR_TAPS = (0, 2, 4, 6)
        POOL_TAPS = (1, 3, 5, 7)
        EARLY = NB + CONV_LAG

        def early(g):
            return isinstance(g, int) and g < EARLY

        SIGN_PARTS = 6
        PART_TAPS = KT * TAPS // SIGN_PARTS

        def sign_part(i):
            return slice(i * PART_TAPS * KT * P, (i + 1) * PART_TAPS * KT * P)

        def sum_banks(g):
            return PS[:, SCR:SCR + KT, 0:BLK] if g < NB else PS[:, CONV:CONV + KT, 0:BLK]

        def rows_of(j):
            return slice(1 + ROWS * j, 1 + ROWS * (j + 1))

        def cols_of(j):
            return slice(BLK * j, BLK * (j + 1))

        def grid(ap):
            return ap.rearrange("p (r c) -> p r c", c=W)

        def conv_block(im, j):
            if j >= CONV_LAG:
                return (im.n - 1, 1 - im.parity, j - CONV_LAG) if im.before else None
            return (im.n - 2, im.parity, j + NB - CONV_LAG) if im.before2 else None

        def last_conv_block(im, j):
            if j >= 1:
                return conv_block(im, j - 1)
            return (im.n - 2, im.parity, NB - 1 - CONV_LAG) if im.before2 else None

        def next_block(im, j):
            if j + 1 < NB:
                return (im.n, im.parity, j + 1) if im.here else None
            return (im.n + 1, 1 - im.parity, 0) if im.after else None

        def norm_block(im, j):
            if j < NB - 2:
                return (im.n, im.parity, j + 2) if im.here else None
            return (im.n + 1, 1 - im.parity, j - (NB - 2)) if im.after else None

        def normalised_low(eng, n, b):
            eng.wait_ge(xh_ready, n * NB + b + 1)
            eng.tensor_tensor(XS[:, 1, :, :].rearrange("p t (r c) -> p t r c", c=W), XN[:, :, rows_of(b), 1:1 + W],
                              XS[:, 0, :, :].rearrange("p t (r c) -> p t r c", c=W), ALU.subtract).then_inc(xl_ready, 1)

        block = ctx.enter_context(nc.Block())

        @block.sync
        def _(sp):
            def image(dram, n):
                return dram[n] if isinstance(n, int) else dram[bass.ds(n, 1)].rearrange("a p t s -> (a p) t s")

            def load_image(src, parity):
                for t in range(KT):
                    sp.dma_start(X[:, parity, t, :], src[:, t, :]).then_inc(x_loaded[t], 16)

            for i in range(2 * KT):
                t, half = divmod(i, 2)
                part = slice(half * PIX // 2, (half + 1) * PIX // 2)
                sp.dma_start(X[:, 0, t, part], x_dram[0, :, t, part]).then_inc(first_loaded[i], 16)
            for dst, src in ((GAVG[:, :], group_avg), (W1F, w1t), (BN[:, :], bn), (W2F[:, :], w2t),
                             (B2[:, 0, :], b2_rows), (SEL[:, :, :], tap_sel), (HSC[:, :], half_scale), (MASK[:, :], low_mask),
                             (IDENT, identity)):
                sp.dma_start(dst, src).then_inc(consts_loaded, 16)
            sp.dma_start(WRAW, conv_w).then_inc(convw_loaded, 16)
            load_image(x_dram[1], 1)

            def step(im):
                for j in range(NB):
                    c = last_conv_block(im, j)
                    if c:
                        n, parity, b = c
                        if later(n):
                            sp.wait_ge(stored[b], n * 16)
                        sp.wait_ge(final_done, (n * NB + b + 1) * KT)
                        sp.dma_start(image(out_dram, n)[:, :, cols_of(b)], X1[:, parity, :, cols_of(b)]).then_inc(stored[b], 16)
                    if j == NB - 2 and im.after2:
                        sp.wait_ge(xh_ready, (im.n + 1) * NB)
                        load_image(image(x_dram, im.n + 2), im.parity)

            iterations(sp, step)
            for b in range(NB):
                sp.wait_ge(stored[b], 16 * B)

        @block.gpsimd
        def _(pool):
            pool.memset(XN[:, :, :, :], 0.0).then_inc(border_ready, 1)
            pool.memset(HL[:, :, :, :, :].rearrange("p h r t c -> p (h r t c)").bitcast(F32), 0.0).then_inc(border_ready, 1)

            def sum_block_early(g, acc, normalised):
                terms = [PROD[:, k % RING, :, :] for k in POOL_TAPS]
                if g > 0:
                    pool.wait_ge(added, g * SUMS)
                pool.wait_ge(prod_done, g * TAPS + POOL_TAPS[1] + 1)
                pool.tensor_tensor(acc, terms[0], terms[1], ALU.add).then_inc(added, 2)
                for i in range(2, len(terms)):
                    pool.wait_ge(added, g * SUMS + i)
                    pool.wait_ge(prod_done, g * TAPS + POOL_TAPS[i] + 1)
                    pool.tensor_tensor(acc, acc, terms[i], ALU.add).then_inc(added, 1)
                    if i == 2:
                        normalised_low(pool, normalised[0], normalised[2])
                pool.wait_ge(added, g * SUMS + len(terms))
                pool.wait_ge(last_ready, g + 1)
                pool.tensor_tensor(acc, acc, LAST, ALU.add).then_inc(added, SUMS - len(terms))

            def sum_abs(i):
                adds = [(WRAW[:, sign_part(0)], WRAW[:, sign_part(i)])]
                if i == SIGN_PARTS - 1:
                    adds += [(WRAW[:, 0:KT * P], WRAW[:, k * KT * P:(k + 1) * KT * P]) for k in range(1, PART_TAPS)]
                pool.wait_ge(abs_ready, i + 1)
                for m, (total, term) in enumerate(adds):
                    if i + m > 1:
                        pool.wait_ge(abs_added, i + m - 1)
                    pool.tensor_tensor(total, total, term, ALU.add).then_inc(abs_added, 1)

            def step(im):
                if not im.here:
                    return
                n, parity = im.n, im.parity
                for j in range(NB):
                    g = n * NB + j
                    acc = X1[:, parity, :, cols_of(j)]
                    if isinstance(n, int) and (n, j) == (1, 0):
                        pool.wait_ge(abs_summed, 1)
                    if early(g):
                        if 1 < j <= SIGN_PARTS and g < NB:
                            sum_abs(j - 1)
                        sum_block_early(g, acc, norm_block(im, j))
                        continue
                    if later(n - 1):
                        pool.wait_ge(stored[j], (n - 1) * 16)
                    for k in range(1, SUMS):
                        if k > 1:
                            pool.wait_ge(added, g * SUMS + k)
                        if k < SUMS - 1:
                            pool.wait_ge(prod_done, g * TAPS + k + 1)
                        else:
                            pool.wait_ge(last_ready, g + 1)
                        pool.tensor_tensor(acc, PROD[:, 0, :, :] if k == 1 else acc, PROD[:, k % RING, :, :], ALU.add
                                           ).then_inc(added, 2 if k == 1 else 1)

            iterations(pool, step)

        @block.scalar
        def _(act):
            def piece_sums(kind, src, piece, before):
                for h, func in enumerate((ACT.Identity, ACT.Square)):
                    junk = JUNK[kind][:, h, :].rearrange("p (a b) -> p a b", b=src.shape[2])
                    if later(before + h - 1):
                        act.wait_ge(sums_ready[kind], before + h - 1)
                    act.activation(junk, src, func, accum_out=PART[:, kind, h, piece:piece + 1]
                                   ).then_inc(sums_ready[kind], 1)

            def x_piece(n, parity, piece):
                t, quarter = divmod(piece, PIECES // KT)
                if quarter == 0:
                    act.wait_ge(x_loaded[t], n * 16)
                size = KT * PIX // PIECES
                src = X[:, parity, t, quarter * size:(quarter + 1) * size].rearrange("p (a b) -> p a b", a=2)
                piece_sums(0, src, piece, (n * PIECES + piece) * 2)

            def x_piece_sum(piece):
                t, quarter = divmod(piece, PIECES // KT)
                if quarter % 2 == 0:
                    act.wait_ge(first_loaded[piece // 2], 16)
                size = KT * PIX // PIECES
                if piece >= 2:
                    act.wait_ge(sums_ready[0], 2 * (piece - 1))
                act.activation(JUNK[0][:, piece % 2, :], X[:, 0, t, quarter * size:(quarter + 1) * size], ACT.Identity,
                               accum_out=PART[:, 0, 0, piece:piece + 1]).then_inc(sums_ready[0], 2)

            def x1_piece(n, parity, b):
                act.wait_ge(added, (n * NB + b + 1) * SUMS)
                if b == 0 and later(n):
                    act.wait_ge(chain[1], (n - 1) * STEPS + 1)
                piece_sums(1, X1[:, parity, :, cols_of(b)], b, (n * NB + b) * 2)

            def normalise(n, parity, b):
                if b == 0 or (b == 1 and isinstance(n, int) and n == 0):
                    act.wait_ge(chain[0], (n + 1) * STEPS)
                last_reader = (n - 1) * NB + min(b + 1, NB - 1) + 1
                if later(last_reader):
                    act.wait_ge(prod_done, last_reader * TAPS)
                act.activation(XN[:, :, rows_of(b), 1:1 + W],
                               X[:, parity, :, cols_of(b)].rearrange("p t (r c) -> p t r c", c=W), ACT.Identity,
                               bias=NORM_UP[:, 0, parity, 1:2], scale=NORM_UP[:, 0, parity, 0:1]).then_inc(xn_ready, 1)

            def normalise_high(n, parity, b):
                if later(n * NB + b):
                    act.wait_ge(hidden_done, n * NB + b)
                act.activation(XS[:, 0, :, :], X[:, parity, :, cols_of(b)], ACT.Identity, bias=NORM_UP[:, 0, parity, 1:2],
                               scale=NORM_UP[:, 0, parity, 0:1]).then_inc(xh_ready, 1)

            def hidden(g, buf):
                act.wait_ge(hidden_done, g + 1)
                if later(g - 1):
                    act.wait_ge(tile_done, (g - 1) * WT)
                act.activation(T[:, buf, :], PS[:, HID, 0:BLK], ACT.Relu, bias=BNF[:, 5:6], scale=BNF[:, 8:9]
                               ).then_inc(u_ready, 1)
                low = PS[MID:P, HID, 0:BLK]
                act.wait_ge(u_ready, 2 * g + 1)
                act.activation(low, low, ACT.Relu, bias=BNF[MID:P, 7:8], scale=BNF[MID:P, 6:7]).then_inc(u_ready, 1)

            def high(g, i, buf):
                act.wait_ge(tile_done, g * WT + i + 1)
                if later(g * WT + i - 1):
                    act.wait_ge(z_ready, g * WT + i - 1)
                act.activation(WH[:, buf, :], PS[0:TPT * WROWS, WTILE, 0:BLK], ACT.Identity,
                               bias=B2[:, 2, i:i + 1], scale=MASK[:, :]).then_inc(high_ready, 1)

            def split(n, parity, b, slot):
                if b == 0:
                    act.wait_ge(chain[1], (n + 1) * STEPS)
                g = n * NB + b
                if later(g):
                    act.wait_ge(low_ready, g)
                act.wait_ge(last_ready, slot)
                last_reader = (n - 1) * NB + min(b + 1, NB - 1) + 1
                if later(last_reader):
                    act.wait_ge(conv_done, last_reader * KT)
                src = X1[:, parity, :, cols_of(b)]
                act.activation(PS[:, SCR:SCR + KT, 0:BLK], src, ACT.Identity, bias=NORM_UP[:, 1, parity, 1:2],
                               scale=NORM_UP[:, 1, parity, 0:1])
                act.activation(HL[:, 0, rows_of(b), :, 1:1 + W].rearrange("p r t c -> p t r c"),
                               src.rearrange("p t (r c) -> p t r c", c=W), ACT.Identity,
                               bias=NORM[:, 1, parity, 1:2], scale=NORM[:, 1, parity, 0:1]).then_inc(split_ready, 1)

            def signs(i):
                part = sign_part(i)
                if i == 0:
                    act.wait_ge(convw_loaded, 16)
                hi, lo = (CW[:, h, :, :, :].rearrange("p t k o -> p (t k o)")[:, part] for h in range(2))
                act.activation(hi, WRAW[:, part], ACT.Sign).then_inc(signs_ready, 1)
                act.wait_ge(signs_ready, 2 * i + 1)
                act.activation(lo, hi, ACT.Identity, scale=1.0 / LOSCALE).then_inc(signs_ready, 1)
                act.activation(WRAW[:, part], WRAW[:, part], ACT.Abs).then_inc(abs_ready, 1)

            def root(kind, n):
                act.wait_ge(chain[kind], n * STEPS + 6)
                act.activation(SD[:, kind:kind + 1], VAR[:, kind:kind + 1], ACT.Sqrt).then_inc(sd_ready[kind], 1)

            act.wait_ge(ones_ready, 1)
            act.activation(SD[:, 1:2], ONES[:, :], ACT.Sqrt)
            for piece in range(PIECES):
                x_piece_sum(piece)
            act.wait_ge(consts_ready, 1)
            act.activation(BNF[:, 1:2], BNF[:, 0:1], ACT.Sqrt).then_inc(bn_sqrt, 1)
            root(0, 0)
            act.wait_ge(border_ready, 1)
            normalise(0, 0, 0)
            normalise_high(0, 0, 0)
            normalise(0, 0, 1)
            act.wait_ge(consts_ready, BN_SETUP)
            hidden(0, 0)
            normalise_high(0, 0, 1)
            act.wait_ge(consts_ready, SETUP)
            act.wait_ge(border_ready, 2)
            for i in range(WT - 1):
                high(0, i, i % 2)

            def step(im):
                for j in range(NB):
                    nxt = next_block(im, j)
                    slot = min(im.n * NB + j, B * NB) if isinstance(im.n, int) else im.n * NB + j
                    if nxt:
                        n, parity, b = nxt
                        g, buf = n * NB + b, (parity + b) % 2
                        hidden(g, buf)
                    if im.here:
                        high(im.n * NB + j, 2, (im.parity + j) % 2)
                    if im.before and j >= 1:
                        split(im.n - 1, 1 - im.parity, j if j > 1 else 0, slot)
                    if norm_block(im, j):
                        normalise(*norm_block(im, j))
                        normalise_high(*norm_block(im, j))
                    if im.before and j == 1:
                        split(im.n - 1, 1 - im.parity, 1, slot)
                    if nxt:
                        high(g, 0, buf)
                    if j >= 1 and im.here:
                        x1_piece(im.n, im.parity, j - 1)
                    if j == 0 and im.before:
                        x1_piece(im.n - 1, 1 - im.parity, NB - 1)
                    if 2 * j < PIECES and im.after:
                        for piece in (2 * j, 2 * j + 1):
                            x_piece(im.n + 1, 1 - im.parity, piece)
                    if nxt:
                        high(g, 1, (buf + 1) % 2)
                    if j == 0 and im.before:
                        root(1, im.n - 1)
                    if j == 4 and im.after:
                        root(0, im.n + 1)
                    if isinstance(im.n, int) and im.n == 0 and j < SIGN_PARTS:
                        signs(j)

            iterations(act, step)

        @block.vector
        def _(dve):
            def link(ins, kind, value):
                ins.then_inc(chain[kind], 1)
                dve.wait_ge(chain[kind], value)

            def channel_stats(kind, n):
                pieces = PIECES if kind == 0 else NB
                dve.wait_ge(sums_ready[kind], (n + 1) * pieces * 2)
                link(dve.tensor_reduce(TOT[:, kind, :], PART[:, kind, :, 0:pieces], mybir.AxisListType.X, ALU.add),
                     kind, n * STEPS + 1)
                dve.tensor_scalar(AGG[:, kind, :], TOT[:, kind, :], 1.0 / (KT * PIX), None, ALU.mult
                                  ).then_inc(chain[kind], 1)

            def group_variance(kind, n):
                s = n * STEPS
                one = slice(kind, kind + 1)
                dve.wait_ge(group_sum[kind], n + 1)
                link(dve.tensor_copy(GRP[:, kind, :], PS[:, HID, STAT]), kind, s + 3)
                link(dve.tensor_tensor(MSQ[:, one], GRP[:, kind, 0:1], GRP[:, kind, 0:1], ALU.mult), kind, s + 4)
                link(dve.tensor_tensor(DIF[:, one], GRP[:, kind, 1:2], MSQ[:, one], ALU.subtract), kind, s + 5)
                dve.tensor_scalar(VAR[:, one], DIF[:, one], 0.0, GN_EPS, ALU.max, ALU.add).then_inc(chain[kind], 1)

            def scale_and_bias(kind, n, parity):
                s = n * STEPS
                one = slice(kind, kind + 1)
                scale, bias = NORM[:, kind, parity, 0:1], NORM[:, kind, parity, 1:2]
                dve.wait_ge(sd_ready[kind], n + 1)
                link(dve.reciprocal(RS0[:, one], SD[:, one]), kind, s + 7)
                link(dve.scalar_tensor_tensor(out=TMP[:, one], in0=RS0[:, one], scalar=RS0[:, one], in1=VAR[:, one],
                                              op0=ALU.mult, op1=ALU.mult), kind, s + 8)
                link(dve.tensor_scalar(MSQ[:, one], TMP[:, one], -0.5, 1.5, ALU.mult, ALU.add), kind, s + 9)
                link(dve.tensor_tensor(scale, RS0[:, one], MSQ[:, one], ALU.mult), kind, s + 10)
                link(dve.scalar_tensor_tensor(out=bias, in0=GRP[:, kind, 0:1], scalar=-1.0, in1=scale,
                                              op0=ALU.mult, op1=ALU.mult), kind, s + 11)
                if kind == 0:
                    dve.scalar_tensor_tensor(out=BACK[:, parity, 0:1], in0=VAR[:, one], scalar=1.0 / XSCALE, in1=scale,
                                             op0=ALU.mult, op1=ALU.mult)
                    dve.tensor_copy(BACK[:, parity, 1:2], GRP[:, kind, 0:1])
                dve.tensor_scalar(NORM_UP[:, kind, parity, :], NORM[:, kind, parity, :], LOSCALE if kind else XSCALE,
                                  None, ALU.mult).then_inc(chain[kind], 1)

            def ring(g, k):
                if early(g) or (isinstance(g, int) and g == EARLY and k < RING):
                    if k in TENSOR_TAPS:
                        if k >= RING:
                            dve.wait_ge(tensor_added, g * len(TENSOR_TAPS) + (k - RING) // 2 + 1)
                    else:
                        count = g * SUMS + POOL_TAPS.index(k) - RING // 2 + 1 if k >= RING else (
                            (g - 1) * SUMS + POOL_TAPS.index(k + RING) + 1)
                        if count > 0:
                            dve.wait_ge(added, count)
                elif later(g * SUMS + k + 1 - RING):
                    dve.wait_ge(added, g * SUMS + k + 1 - RING)

            def product(g, parity, j, k):
                dve.wait_ge(bcast_done, g * TAPS + k + 1)
                di, dj = divmod(k, 3)
                shifted = XN[:, :, ROWS * j + di:ROWS * j + di + ROWS, dj:dj + W]
                weights = grid(PS[:, BCAST + (parity + j + k) % 2, 0:BLK])
                if k == TAPS - 1 and early(g):
                    dst = LAST
                elif k == TAPS - 1:
                    dst = PS[:, SCR:SCR + KT, 0:BLK]
                else:
                    dst = PROD[:, k % RING, :, :]
                dst = dst.rearrange("p t (r c) -> p t r c", c=W)
                if k == TAPS // 2:
                    for t in range(KT):
                        ins = dve.scalar_tensor_tensor(out=dst[:, t], in0=weights, scalar=BACK[:, parity, 0:1],
                                                       in1=shifted[:, t], op0=ALU.add, op1=ALU.mult)
                else:
                    both = weights.rearrange("p (t r) c -> p t r c", t=1).to_broadcast([P, KT, ROWS, W])
                    ins = dve.tensor_tensor(dst, both, shifted, ALU.mult)
                ins.then_inc(prod_done, 1)

            def final_term(g, parity, dst, part):
                dve.wait_ge(prod_done, (g + 1) * TAPS)
                dve.scalar_tensor_tensor(out=dst, in0=part, scalar=BACK[:, parity, 1:2], in1=dst, op0=ALU.add, op1=ALU.add
                                         ).then_inc(last_ready, 1)

            def low_activations(g, buf):
                dve.wait_ge(u_ready, 2 * g + 2)
                low = T[MID:P, buf, :]
                dve.scalar_tensor_tensor(out=low, in0=low, scalar=-LOSCALE, in1=PS[MID:P, HID, 0:BLK],
                                         op0=ALU.mult, op1=ALU.add).then_inc(t_ready, 1)

            def low_rows(g, i, buf):
                dve.wait_ge(high_ready, g * WT + i + 1)
                dve.scalar_tensor_tensor(out=WZ[:, buf, i, :], in0=PS[0:TPT * WROWS, WTILE, 0:BLK], scalar=B2[:, 1, i:i + 1],
                                         in1=WH[:, (buf + i) % 2, :], op0=ALU.add, op1=ALU.subtract).then_inc(z_ready, 1)

            def low_half(n, b):
                dve.wait_ge(split_ready, n * NB + b + 1)
                for t in range(KT):
                    ins = dve.scalar_tensor_tensor(out=HL[:, 1, rows_of(b), t, 1:1 + W], in0=HL[:, 0, rows_of(b), t, 1:1 + W],
                                                   scalar=-LOSCALE, in1=grid(PS[:, SCR + t, 0:BLK]), op0=ALU.mult, op1=ALU.add)
                ins.then_inc(low_ready, 1)

            def residual(n, parity, b, t):
                dve.wait_ge(conv_done, (n * NB + b) * KT + t + 1)
                o = X1[:, parity, t, cols_of(b)]
                dve.scalar_tensor_tensor(out=o, in0=PS[:, CONV + t, 0:BLK], scalar=CSC[:, t:t + 1], in1=o,
                                         op0=ALU.mult, op1=ALU.add).then_inc(final_done, 1)

            def setup(ins, value=None):
                ins.then_inc(consts_ready, 1)
                if value:
                    dve.wait_ge(consts_ready, value)

            dve.memset(ONES[:, :], 1.0).then_inc(ones_ready, 1)
            for piece in range(PIECES):
                t, quarter = divmod(piece, PIECES // KT)
                if quarter % 2 == 0:
                    dve.wait_ge(first_loaded[piece // 2], 16)
                size = KT * PIX // PIECES
                src = X[:, 0, t, quarter * size:(quarter + 1) * size]
                dve.scalar_tensor_tensor(out=X1[:, 0, t, quarter * size:(quarter + 1) * size], in0=src, scalar=1.0, in1=src,
                                         op0=ALU.mult, op1=ALU.mult, accum_out=PART[:, 0, 1, piece:piece + 1]
                                         ).then_inc(squares_ready, 1)
            dve.wait_ge(consts_loaded, 16 * CONSTS)
            setup(dve.tensor_scalar(BNF[:, 0:1], BN[:, 3:4], BN_EPS, None, ALU.add))
            dve.wait_ge(squares_ready, PIECES)
            channel_stats(0, 0)
            group_variance(0, 0)
            scale_and_bias(0, 0, 0)
            setup(dve.tensor_scalar(W1F, W1F, W1SCALE, None, ALU.mult), 2)
            setup(dve.tensor_copy(W1[:, 0, :, :], W1F), 3)
            setup(dve.tensor_tensor(W1[:, 1, :, :], W1F, W1[:, 0, :, :], ALU.subtract))
            dve.wait_ge(bn_sqrt, 1)
            setup(dve.reciprocal(BNF[:, 2:3], BNF[:, 1:2]), 5)
            setup(dve.tensor_tensor(BNF[:, 3:4], BN[:, 0:1], BNF[:, 2:3], ALU.mult), 6)
            setup(dve.tensor_tensor(BNF[:, 4:5], BN[:, 2:3], BNF[:, 3:4], ALU.mult), 7)
            setup(dve.tensor_tensor(BNF[:, 5:6], BN[:, 1:2], BNF[:, 4:5], ALU.subtract), 8)
            setup(dve.tensor_scalar(BNF[:, 8:9], BNF[:, 3:4], 1.0 / (XSCALE * W1SCALE), None, ALU.mult))
            setup(dve.tensor_scalar(BNF[:, 6:7], BNF[:, 3:4], LOSCALE / (XSCALE * W1SCALE), None, ALU.mult))
            setup(dve.tensor_scalar(BNF[:, 7:8], BNF[:, 5:6], LOSCALE, None, ALU.mult))
            normalised_low(dve, 0, 0)
            setup(dve.tensor_scalar(W2F[:, :], W2F[:, :], WSCALE, None, ALU.mult), 12)
            setup(dve.tensor_copy(W2[:, 0, :], W2F[:, :]), 13)
            setup(dve.tensor_tensor(W2D[:, :], W2F[:, :], W2[:, 0, :], ALU.subtract), 14)
            setup(dve.tensor_scalar(W2[:, 1, :], W2D[:, :], HSC[:, :], None, ALU.mult))
            setup(dve.tensor_scalar(W2[:, 0, :], W2[:, 0, :], HSC[:, :], None, ALU.mult))
            setup(dve.tensor_scalar(B2[:, 1, :], B2[:, 0, :], WSCALE, None, ALU.mult), 17)
            setup(dve.tensor_scalar(B2[:, 2, :], B2[:, 1, :], MASK[:, :], None, ALU.mult))
            low_activations(0, 0)
            normalised_low(dve, 0, 1)
            low_rows(0, 0, 0)

            def channel_scales():
                dve.wait_ge(abs_summed, 1)
                for t in range(KT):
                    ins = dve.tensor_scalar(CSC[:, t:t + 1], PS[:, CONV + t, 0:1], 1.0 / (KT * P * TAPS), None, ALU.mult)
                ins.then_inc(scales_ready, 1)

            def step(im):
                n, parity = im.n, im.parity
                for j in range(NB):
                    nxt = next_block(im, j)
                    if nxt:
                        next_g, buf = nxt[0] * NB + nxt[2], (nxt[1] + nxt[2]) % 2
                    for k in range(TAPS):
                        if im.here:
                            g = n * NB + j
                            if k == 0:
                                dve.wait_ge(xn_ready, n * NB + min(j + 1, NB - 1) + 1)
                            if k < TAPS - 1:
                                ring(g, k)
                            if k == TAPS - 1 and early(g) and g > 0:
                                dve.wait_ge(added, g * SUMS)
                            split_so_far = (n - 1) * NB + (j + 1 if j else 0)
                            if k == TAPS - 1 and not early(g) and later(split_so_far):
                                dve.wait_ge(low_ready, split_so_far)
                            product(g, parity, j, k)
                        if isinstance(n, int) and (n, j, k) == (1, 0, 0):
                            channel_scales()
                        if k == 0 and j == 1 and im.before:
                            scale_and_bias(1, n - 1, 1 - parity)
                        if k == 0 and im.here:
                            low_rows(g, 1, (parity + j) % 2)
                        if k == 1 and last_conv_block(im, j):
                            residual(*last_conv_block(im, j), 1)
                        if k == 2 and nxt:
                            low_activations(next_g, buf)
                        if k == 2 and j == 4 and im.after:
                            channel_stats(0, n + 1)
                        if k == 3 and im.here:
                            low_rows(g, 2, (parity + j) % 2)
                        if k == 4 and j >= 1 and im.before:
                            low_half(n - 1, j if j > 1 else 0)
                        if k == 5 and conv_block(im, j):
                            residual(*conv_block(im, j), 0)
                        if k == 6 and nxt:
                            low_rows(next_g, 0, buf)
                        if k == 7 and j == 1 and im.before:
                            low_half(n - 1, 1)
                        if k == 7 and norm_block(im, j) and not early(n * NB + j):
                            normalised_low(dve, norm_block(im, j)[0], norm_block(im, j)[2])
                        if k == 7 and j == 4 and im.after:
                            group_variance(0, n + 1)
                        if k == 6 and j == 0 and im.before:
                            channel_stats(1, n - 1)
                        if k == 8 and j == 0 and im.before:
                            group_variance(1, n - 1)
                        if k == 8 and im.here and early(g):
                            dve.wait_ge(tensor_added, (g + 1) * len(TENSOR_TAPS))
                            final_term(g, parity, LAST, sum_banks(g))
                        elif k == 8 and im.here:
                            final_term(g, parity, PROD[:, (TAPS - 2) % RING, :, :], PS[:, SCR:SCR + KT, 0:BLK])
                        if k == 8 and j == 4 and im.after:
                            scale_and_bias(0, n + 1, 1 - parity)

            iterations(dve, step)

        @block.tensor
        def _(pe):
            HIDDEN_PASSES = [(h, t, hx) for h, hx in ((0, 0), (1, 0), (0, 1)) for t in range(KT)]

            def hidden(n, b):
                g = n * NB + b
                pe.wait_ge(xh_ready, g + 1)
                if later(g):
                    pe.wait_ge(t_ready, g)
                for i, (h, t, hx) in enumerate(HIDDEN_PASSES):
                    if (hx, t) == (1, 0):
                        pe.wait_ge(xl_ready, g + 1)
                    ins = pe.matmul(PS[:, HID, 0:BLK], W1[:, h, t, :], XS[:, hx, t, :],
                                    start=i == 0, stop=i == len(HIDDEN_PASSES) - 1)
                ins.then_inc(hidden_done, 1)

            def weight_tile(g, i, buf):
                if i == 0:
                    pe.wait_ge(t_ready, g + 1)
                if later(g * WT + i):
                    pe.wait_ge(z_ready, g * WT + i)
                for h in range(2):
                    ins = pe.matmul(PS[0:TPT * WROWS, WTILE, 0:BLK], W2[:, h, TPT * WROWS * i:TPT * WROWS * (i + 1)],
                                    T[:, buf, :], start=h == 0, stop=h == 1)
                ins.then_inc(tile_done, 1)

            def broadcast(g, buf, k):
                if k % TPT == 0:
                    pe.wait_ge(z_ready, g * WT + k // TPT + 1)
                last_use = g * TAPS + k - 1
                if later(last_use):
                    pe.wait_ge(prod_done, last_use)
                pe.matmul(PS[:, BCAST + (buf + k) % 2, 0:BLK], SEL[:, k % TPT, :], WZ[:, buf, k // TPT, :],
                          start=True, stop=True).then_inc(bcast_done, 1)

            MIDDLE = TAPS // 2
            tile_order = [(t, k, h) for t in range(KT) for k in range(TAPS) if k != MIDDLE for h in range(2)]
            tile_order = [(0, MIDDLE, 0), (0, MIDDLE, 1)] + tile_order + [(KT - 1, MIDDLE, 0), (KT - 1, MIDDLE, 1)]
            conv_order = [(o, t, k, h) for o in range(KT) for t, k, h in tile_order]
            per_tap = len(conv_order) // TAPS

            def convolve(n, b, part):
                for o, t, k, h in conv_order[per_tap * part:per_tap * (part + 1)]:
                    first, last = (t, k, h) == tile_order[0], (t, k, h) == tile_order[-1]
                    if first and o == 0 and isinstance(n, int) and (n, b) == (0, 0):
                        pe.wait_ge(last_ready, EARLY)
                    if first and o == 0:
                        pe.wait_ge(low_ready, n * NB + min(b + 1, NB - 1) + 1)
                    if first and later((n * NB + b) * KT + o - 1):
                        pe.wait_ge(final_done, (n * NB + b) * KT + o - 1)
                    di, dj = divmod(k, 3)
                    r0 = 1 if b == 0 and di == 0 else 0
                    r1 = ROWS - 1 if b == NB - 1 and di == 2 else ROWS
                    c0, c1 = (1 if dj == 0 else 0), (W - 1 if dj == 2 else W)
                    ins = pe.matmul(grid(PS[:, CONV + o, 0:BLK])[:, r0:r1, c0:c1], CW[:, h, t, k, P * o:P * (o + 1)],
                                    HL[:, h, ROWS * b + di + r0:ROWS * b + di + r1, t, dj + c0:dj + c1],
                                    start=first, stop=last)
                    if last:
                        ins.then_inc(conv_done, 1)

            def sum_weights():
                pe.wait_ge(ones_ready, 1)
                pe.wait_ge(abs_added, SIGN_PARTS - 1 + PART_TAPS - 1)
                for o in range(KT):
                    ins = pe.matmul(PS[:, CONV + o, 0:1], WRAW[:, P * o:P * (o + 1)], ONES[:, :], start=True, stop=True)
                ins.then_inc(abs_summed, 1)

            def group_average(kind, n):
                pe.wait_ge(chain[kind], n * STEPS + 2)
                pe.matmul(PS[:, HID, STAT], GAVG[:, :], AGG[:, kind, :], start=True, stop=True).then_inc(group_sum[kind], 1)

            def add_product(g, k, t):
                if (g, k, t) == (NB, TENSOR_TAPS[0], 0):
                    pe.wait_ge(scales_ready, 1)
                if k == TENSOR_TAPS[0] and t == 0 and g > 0:
                    pe.wait_ge(last_ready, g)
                pe.wait_ge(prod_done, g * TAPS + k + 1)
                ins = pe.matmul(sum_banks(g)[:, t, :], IDENT, PROD[:, k % RING, t, :],
                                start=k == TENSOR_TAPS[0], stop=k == TENSOR_TAPS[-1])
                if t == KT - 1:
                    ins.then_inc(tensor_added, 1)

            pe.wait_ge(consts_loaded, 16 * CONSTS)
            group_average(0, 0)
            pe.wait_ge(consts_ready, W1_SETUP)
            pe.wait_ge(chain[0], 3)
            hidden(0, 0)
            pe.wait_ge(consts_ready, SETUP)
            weight_tile(0, 0, 0)

            def step(im):
                n, parity = im.n, im.parity
                for j in range(NB):
                    nxt = next_block(im, j)
                    for k in range(TAPS):
                        if im.here:
                            broadcast(n * NB + j, (parity + j) % 2, k)
                        if im.here and early(n * NB + j) and k - 2 in TENSOR_TAPS:
                            add_product(n * NB + j, k - 2, 0)
                            if k == TAPS - 1:
                                add_product(n * NB + j, k - 2, 1)
                        if im.here and early(n * NB + j) and k - 3 in TENSOR_TAPS:
                            add_product(n * NB + j, k - 3, 1)
                        c = conv_block(im, j)
                        if c:
                            convolve(c[0], c[2], k)
                        if isinstance(n, int) and (n, j, k) == (0, NB - 1, TAPS - 1):
                            sum_weights()
                        if k == 0 and isinstance(n, int) and n == 0 and j == 0:
                            weight_tile(0, 1, 0)
                        if k == 1 and im.here:
                            weight_tile(n * NB + j, 2, (parity + j) % 2)
                        if k == 0 and nxt:
                            if j == 1 and im.before:
                                pe.wait_ge(chain[1], (n - 1) * STEPS + 3)
                            if j == 5 and im.after:
                                pe.wait_ge(chain[0], (n + 1) * STEPS + 3)
                            hidden(nxt[0], nxt[2])
                        if k in (4, 8) and nxt:
                            weight_tile(nxt[0] * NB + nxt[2], k // 4 - 1, (nxt[1] + nxt[2]) % 2)
                        if k == 4 and j == 4 and im.after:
                            pe.wait_ge(t_ready, n * NB + j + 2)
                            group_average(0, n + 1)
                        if k == 7 and j == 0 and im.before:
                            if im.here:
                                pe.wait_ge(t_ready, n * NB + j + 2)
                            group_average(1, n - 1)

            iterations(pe, step)


def kernel(x, L0_conv_w1, L0_conv_bn_gamma, L0_conv_bn_beta, L0_conv_bn_mean, L0_conv_bn_var, L0_conv_w2,
           L0_conv_b2, L1_conv_weights):
    import numpy as np
    import concourse.bacc as bacc
    from concourse.bass_utils import run_bass_kernel_spmd

    x = np.ascontiguousarray(x)
    B, C = x.shape[:2]
    w1, w2, b2, wc = (np.asarray(a) for a in (L0_conv_w1, L0_conv_w2, L0_conv_b2, L1_conv_weights))
    w2k = w2.T.reshape(MID, GROUPS, TAPS).transpose(0, 2, 1)
    w2k = np.stack([w2k, w2k], axis=2).reshape(MID, TAPS * WROWS)
    b2k = b2.reshape(GROUPS, TAPS).T
    b2k = np.stack([b2k, b2k], axis=1).reshape(WT, TPT * WROWS).T
    w1t = w1.T.reshape(P, KT, MID)
    bn = np.stack([np.asarray(a) for a in (L0_conv_bn_gamma, L0_conv_bn_beta, L0_conv_bn_mean, L0_conv_bn_var)], axis=1)
    sel = np.zeros((TPT, 2, GROUPS, TPT, P), np.float16)
    for k in range(TPT):
        for g in range(GROUPS):
            sel[k, :, g, k, P // GROUPS * g:P // GROUPS * (g + 1)] = 1.0 / (WSCALE * XSCALE)
    half_scale = np.repeat(np.float32([1.0, 1.0 / LOSCALE]), MID)[:, None]
    low_mask = np.tile(np.repeat(np.float32([0.0, 1.0]), GROUPS), TPT)[:, None]
    arrays = {
        "x_dram": x.reshape(B, C, PIX),
        "w1t_dram": np.ascontiguousarray(np.concatenate([w1t, w1t], axis=2)),
        "bn_dram": np.ascontiguousarray(np.concatenate([bn, bn], axis=0)),
        "w2t_dram": np.ascontiguousarray(np.concatenate([w2k, w2k], axis=0)),
        "b2_dram": np.ascontiguousarray(b2k),
        "conv_w_dram": np.ascontiguousarray(
            wc.reshape(P, KT, P, KT, TAPS).transpose(2, 3, 4, 1, 0).reshape(P, KT * TAPS * KT * P)),
        "sel_dram": sel.reshape(TPT * WROWS, TPT, P),
        "group_avg_dram": np.kron(np.eye(P // 4), np.full((4, 4), 1 / 4)).astype(np.float32),
        "identity_dram": np.eye(P, dtype=np.float32),
        "half_scale_dram": np.ascontiguousarray(half_scale),
        "low_mask_dram": np.ascontiguousarray(low_mask),
    }
    nc = bacc.Bacc("TRN2", target_bir_lowering=False, num_devices=1)
    aps = [nc.dram_tensor(k, a.shape, mybir.dt.from_np(a.dtype), kind="ExternalInput").ap() for k, a in arrays.items()]
    out = nc.dram_tensor("out_dram", (B, C, PIX), F32, kind="ExternalOutput").ap()
    program(nc, *aps, out)
    r = run_bass_kernel_spmd(nc, [arrays], core_ids=[0])
    return r.results[0]["out_dram"].reshape(x.shape)
```
